# Optimizing a Trainium2 kernel written in Bass

```python
import numpy as np
import jax
import jax.numpy as jnp

def _softmax(x, axis=-1):
    return jax.nn.softmax(x, axis=axis)

def _gelu(x):
    return jax.nn.gelu(x, approximate=True)

def _silu(x):
    return jax.nn.silu(x)

def _sigmoid(x):
    return jax.nn.sigmoid(x)

def _layernorm(x, axis=-1, eps=1e-05):
    m = jnp.mean(x, axis=axis, keepdims=True)
    v = jnp.var(x, axis=axis, keepdims=True)
    return (x - m) / jnp.sqrt(v + eps)

def _scatter_add(tgt, idx, src, axis=0):
    return tgt.at[idx].add(src)

def _segment_sum(src, seg, n):
    return jax.ops.segment_sum(src, seg, n)
kernel_name = 'mk_macaron_d1_jaxref_r8_ca2da3'

def setup_inputs(seed: int=0):
    np.random.seed(seed)
    _w = jnp.asarray

    def _L0_attn_setup():
        import jax, jax.numpy as jnp
        import numpy as np
        HEADS = 16

        def _split_heads(t, h):
            b, y, hd = t.shape
            d = hd // h
            return t.reshape(b, y, h, d).transpose(0, 2, 1, 3).reshape(b * h, y, d)

        def _merge_heads(t, b, h):
            bh, y, d = t.shape
            return t.reshape(b, h, y, d).transpose(0, 2, 1, 3).reshape(b, y, h * d)
        key = jax.random.key(seed)
        ks = jax.random.split(key, 5)
        B, S, D = (8, 512, 128)
        scale = 1.0 / np.sqrt(D)
        x = jax.random.normal(ks[0], (B, S, D), dtype=jnp.float32)
        Wq = jax.random.normal(ks[1], (D, D), dtype=jnp.float32) * scale
        Wk = jax.random.normal(ks[2], (D, D), dtype=jnp.float32) * scale
        Wv = jax.random.normal(ks[3], (D, D), dtype=jnp.float32) * scale
        Wo = jax.random.normal(ks[4], (D, D), dtype=jnp.float32) * scale
        return {'x': x, 'Wq': Wq, 'Wk': Wk, 'Wv': Wv, 'Wo': Wo}
    _L0_attn_in = _L0_attn_setup()

    def _L0_ffn_setup():
        import jax, jax.numpy as jnp
        import numpy as np
        B, S, DIM = (4, 256, 128)
        E, K, HID = (8, 2, 512)
        key = jax.random.key(seed)
        ks = jax.random.split(key, 8)
        init = lambda k, sh: jax.random.normal(k, sh, jnp.float32) * 0.02
        return {'x': jax.random.normal(ks[0], (B, S, DIM), jnp.float32), 'gate_w': init(ks[1], (DIM, E)), 'gate_b': jnp.zeros((E,), jnp.float32), 'w1': init(ks[2], (E, DIM, HID)), 'b1': jnp.zeros((E, HID), jnp.float32), 'w2': init(ks[3], (E, HID, DIM)), 'b2': jnp.zeros((E, DIM), jnp.float32), 'ws1': init(ks[4], (DIM, HID)), 'bs1': jnp.zeros((HID,), jnp.float32), 'ws2': init(ks[5], (HID, DIM)), 'bs2': jnp.zeros((DIM,), jnp.float32)}
    _L0_ffn_in = _L0_ffn_setup()
    _d = {'L0_attn_x': _L0_attn_in['x'], 'L0_attn_Wq': _L0_attn_in['Wq'], 'L0_attn_Wk': _L0_attn_in['Wk'], 'L0_attn_Wv': _L0_attn_in['Wv'], 'L0_attn_Wo': _L0_attn_in['Wo'], 'L0_ffn_gate_w': _L0_ffn_in['gate_w'], 'L0_ffn_gate_b': _L0_ffn_in['gate_b'], 'L0_ffn_w1': _L0_ffn_in['w1'], 'L0_ffn_b1': _L0_ffn_in['b1'], 'L0_ffn_w2': _L0_ffn_in['w2'], 'L0_ffn_b2': _L0_ffn_in['b2'], 'L0_ffn_ws1': _L0_ffn_in['ws1'], 'L0_ffn_bs1': _L0_ffn_in['bs1'], 'L0_ffn_ws2': _L0_ffn_in['ws2'], 'L0_ffn_bs2': _L0_ffn_in['bs2']}
    _x0 = _d['L0_attn_x']
    _d['L0_attn_x'] = jax.random.normal(jax.random.fold_in(jax.random.key(seed), 1), (32, 256, 128), dtype=_x0.dtype)
    del _x0
    return _d

def reference(L0_attn_x, L0_attn_Wq, L0_attn_Wk, L0_attn_Wv, L0_attn_Wo, L0_ffn_gate_w, L0_ffn_gate_b, L0_ffn_w1, L0_ffn_b1, L0_ffn_w2, L0_ffn_b2, L0_ffn_ws1, L0_ffn_bs1, L0_ffn_ws2, L0_ffn_bs2):

    def _L0_attn_ref(x, Wq, Wk, Wv, Wo):
        import jax, jax.numpy as jnp
        import numpy as np
        HEADS = 16

        def _split_heads(t, h):
            b, y, hd = t.shape
            d = hd // h
            return t.reshape(b, y, h, d).transpose(0, 2, 1, 3).reshape(b * h, y, d)

        def _merge_heads(t, b, h):
            bh, y, d = t.shape
            return t.reshape(b, h, y, d).transpose(0, 2, 1, 3).reshape(b, y, h * d)
        b = x.shape[0]
        h = HEADS
        q = _split_heads(x @ Wq.T, h)
        k = _split_heads(x @ Wk.T, h)
        v = _split_heads(x @ Wv.T, h)
        d = q.shape[-1]
        z = jnp.einsum('byq,byk->bkq', q, k) / jnp.sqrt(jnp.asarray(d, x.dtype))
        z = jax.nn.softmax(z, axis=-1)
        z = jnp.einsum('byz,bvy->bvz', z, v)
        z = _merge_heads(z, b, h)
        return z @ Wo.T

    def _L0_ffn_ref(x, gate_w, gate_b, w1, b1, w2, b2, ws1, bs1, ws2, bs2):
        import jax, jax.numpy as jnp
        import numpy as np
        B, S, DIM = (4, 256, 128)
        E, K, HID = (8, 2, 512)
        orig_shape = x.shape
        xf = x.reshape(-1, DIM)
        logits = xf @ gate_w + gate_b
        top_w, top_i = jax.lax.top_k(logits, K)
        gw = jax.nn.softmax(top_w, axis=-1).astype(xf.dtype)
        combine = (gw[:, :, None] * jax.nn.one_hot(top_i, E, dtype=xf.dtype)).sum(axis=1)
        out = jnp.zeros_like(xf)
        for e in range(E):
            h = jax.nn.gelu(xf @ w1[e] + b1[e], approximate=False)
            out = out + combine[:, e:e + 1] * (h @ w2[e] + b2[e])
        shared = jax.nn.gelu(xf @ ws1 + bs1, approximate=False) @ ws2 + bs2
        return (out + shared).reshape(orig_shape)
    x = L0_attn_x
    x = x + 0.5 * _L0_ffn_ref(_layernorm(x, axis=-1), L0_ffn_gate_w, L0_ffn_gate_b, L0_ffn_w1, L0_ffn_b1, L0_ffn_w2, L0_ffn_b2, L0_ffn_ws1, L0_ffn_bs1, L0_ffn_ws2, L0_ffn_bs2)
    x = x + _L0_attn_ref(_layernorm(x, axis=-1), L0_attn_Wq, L0_attn_Wk, L0_attn_Wv, L0_attn_Wo)
    x = x + 0.5 * _L0_ffn_ref(_layernorm(x, axis=-1), L0_ffn_gate_w, L0_ffn_gate_b, L0_ffn_w1, L0_ffn_b1, L0_ffn_w2, L0_ffn_b2, L0_ffn_ws1, L0_ffn_bs1, L0_ffn_ws2, L0_ffn_bs2)
    return x

_drawn_inputs = setup_inputs


def setup_inputs(seed=0):
    import zlib

    import numpy as np

    out = dict(_drawn_inputs(seed))
    spreads = {'L0_ffn_gate_b': (0.0, 0.1),
     'L0_ffn_b1': (0.0, 0.416),
     'L0_ffn_b2': (0.0, 0.1),
     'L0_ffn_bs1': (0.0, 0.317),
     'L0_ffn_bs2': (0.0, 0.1)}
    factors = {}
    for name, (base, spread) in spreads.items():
        noise = np.random.default_rng([zlib.crc32(name.encode()), seed]).standard_normal(out[name].shape)
        drawn = base * np.exp(spread * noise) if base else spread * noise
        out[name] = jnp.asarray(drawn.astype(out[name].dtype))
    for name, factor in factors.items():
        out[name] = (out[name] * factor).astype(out[name].dtype)
    return out
```

```python
from contextlib import ExitStack

import numpy as np

import concourse.bass as bass
from concourse import mybir

F32 = mybir.dt.float32
BF16 = mybir.dt.bfloat16
I32 = mybir.dt.int32
ALU = mybir.AluOpType
ACT = mybir.ActivationFunctionType
AX = mybir.AxisListType

P = 128
HEAD = 8
EPS = 1e-5
BIG = 3.0e38

TILES = 4
CHUNK = TILES * P
BLOCK = 256
STEPS = 7
AHEAD = 5
FREE = 6

GELU_SLOT = [0, 1, 0, 1, 0, 1, 2]
HBANK = [0, 1, 2, 0, 1, 2, 0, 1, 2, 0, 1, 2, 0, 1]
YBANK = [0, 1, 0, 1, 0, 1, 0]


def back(pattern, at):
    n = len(pattern)
    return next(d for d in range(1, n + 1) if pattern[(at - d) % n] == pattern[at])


def macaron_block(nc, x, wq, wk, wv, wo, gate_w, gate_b, w1, b1, w2, b2, ws1, bs1, ws2, bs2, out):
    batch, seq, dim = x.shape
    experts, _, hidden = w1.shape
    HC = hidden // P
    NX = experts + 1
    SH = experts
    tokens = batch * seq
    groups = 2
    chunks = tokens // CHUNK
    per_group = chunks // groups
    gtok = tokens // groups
    SHARED = gtok // BLOCK
    ROUTED = (2 * gtok - experts) // BLOCK + experts
    NB = per_group * STEPS
    RT = NB - SHARED
    assert RT >= ROUTED and dim == P and seq == 2 * P and HC == 4
    CAP = gtok + BLOCK
    DUMMY = experts * CAP
    SROW = DUMMY + BLOCK
    NR = SROW + gtok
    NE = 4 * NB + 8
    E_BASE = float(np.exp(1.0))
    EXP_BASE = float(np.exp(1.0 / np.sqrt(HEAD)))

    with ExitStack() as ctx:
        def sb(name, shape, dt=F32):
            return ctx.enter_context(nc.sbuf_tensor(name, shape, dt))

        def sem(name):
            return ctx.enter_context(nc.semaphore(name))

        def psum(name, shape, dt=F32):
            return ctx.enter_context(nc.psum_tensor(name, shape, dt))

        xbuf = nc.dram_tensor("slots_in", [4 * NR, 2 * P], BF16, kind="Internal").ap()
        ybuf = [nc.dram_tensor(f"slots_out{g}", [NB * BLOCK, P], F32, kind="Internal").ap() for g in range(groups)]

        X = sb("X", [P, chunks * TILES, P])
        w1h = sb("w1h", [P, NX, hidden], BF16)
        w1l = sb("w1l", [P, NX, hidden], BF16)
        w2h = sb("w2h", [P, NX, HC * P], BF16)
        w2l = sb("w2l", [P, NX, HC * P], BF16)
        b2p = sb("b2p", [P, NX * P], BF16)
        b1row = sb("b1row", [NX * HC, P])
        b1t = sb("b1t", [P, NX * HC])
        wst = sb("wst", [P, 2, 2, hidden])
        b2f = sb("b2f", [1, 4, NX * P])
        b2s = sb("b2s", [1, 3, NX * P], BF16)
        watt = sb("watt", [P, 4, P])
        wqT = sb("wqT", [P, P])
        wkT = sb("wkT", [P, P])
        woT = sb("woT", [P, P])
        gw = sb("gw", [P, experts])
        gb = sb("gb", [P, experts])
        idf = sb("idf", [P, P])
        idb = sb("idb", [P, P], BF16)
        onesb = sb("onesb", [P, P], BF16)
        upper = sb("upper", [P, P], BF16)
        sel3 = sb("sel3", [P, P], BF16)
        mask = sb("mask", [P, P])
        rev = sb("rev", [P, experts])
        ecap = sb("ecap", [P, experts])
        mhalf = sb("mhalf", [P, TILES])
        ebase = sb("ebase", [P, TILES])
        expbase = sb("expbase", [P, 2 * HEAD])
        tri = sb("tri", [1, experts, experts])
        nidx = sb("nidx", [1, RT])
        zero = sb("zero", [P, 2, 2 * P], BF16)
        xin = sb("xin", [P, STEPS, 2, 2 * P], BF16)
        xT = sb("xT", [P, STEPS, 2, BLOCK], BF16)
        g32 = sb("g32", [P, 3, HC, BLOCK])
        gh = sb("gh", [P, 3, HC, BLOCK], BF16)
        gl = sb("gl", [P, 3, HC, BLOCK], BF16)
        yout = sb("yout", [P, STEPS, 2, P])
        etab = sb("etab", [1, NE], I32)
        rtab = sb("rtab", [1, NE], I32)
        st6 = sb("st6", [P, TILES, 6])
        mv = sb("mv", [P, TILES, 2])
        ve = sb("ve", [P, TILES])
        rstd = sb("rstd", [P, TILES])
        xn = sb("xn", [P, TILES, P])
        xnT = sb("xnT", [P, CHUNK])
        xhl = sb("xhl", [P, TILES, 2 * P], BF16)
        lg = sb("lg", [P, TILES, experts])
        lg2 = sb("lg2", [P, TILES, experts])
        cand = sb("cand", [P, TILES, experts])
        m12 = sb("m12", [P, 2, TILES])
        first = sb("first", [P, TILES])
        oh = sb("oh", [P, 2, TILES, experts])
        assign = sb("assign", [P, TILES, experts], BF16)
        asum = sb("asum", [P, experts], BF16)
        arow = sb("arow", [P, experts])
        dlog = sb("dlog", [P, TILES])
        edl = sb("edl", [P, TILES])
        den = sb("den", [P, TILES])
        rden = sb("rden", [P, TILES])
        rk = sb("rk", [P, TILES, experts])
        pick = sb("pick", [P, 2, TILES, experts])
        idx = sb("idx", [P, 2 * TILES], I32)
        pos = sb("pos", [P, per_group, 2 * TILES])
        posge = sb("posge", [P, per_group * 2 * TILES, experts])
        shift = sb("shift", [P, per_group * 2 * TILES])
        hop = sb("hop", [P, experts])
        gix = sb("gix", [P, chunks, 2 * TILES], I32)
        gidx = sb("gidx", [P, 2 * TILES], I32)
        wts = sb("wts", [P, 2, chunks * TILES])
        yg = sb("yg", [P, 2 * TILES, P])
        ysh = sb("ysh", [P, TILES, P])
        gram = sb("gram", [P, 2, P])
        gA = sb("gA", [P, 2, P])
        gm = sb("gm", [P, 2, P])
        hd = sb("hd", [P, 2, HEAD])
        hd2 = sb("hd2", [P, 2, HEAD])
        hmx = sb("hmx", [P, 2])
        hex_ = sb("hex", [P, 2, HEAD])
        hsum = sb("hsum", [P, 2])
        hrec = sb("hrec", [P, 2])
        hp = sb("hp", [P, 2, HEAD])
        prob = sb("prob", [P, 2, P])
        cT = sb("cT", [P, 2, P])
        weff = sb("weff", [P, 2, P])
        cnt = sb("cnt", [P, experts])
        padf = sb("padf", [1, experts])
        padrow = sb("padrow", [1, experts], I32)
        cnt_i = sb("cnt_i", [P, experts], I32)
        nb_i = sb("nb_i", [P, experts], I32)
        nb = sb("nb", [P, experts])
        cumm = sb("cumm", [1, experts, experts])
        cum = sb("cum", [1, experts])
        le = sb("le", [1, RT, experts])
        le2 = sb("le2", [1, RT, experts])
        en = sb("en", [1, RT])
        cp = sb("cp", [1, RT])
        bi = sb("bi", [1, RT])
        ok = sb("ok", [1, RT])
        bo = sb("bo", [1, RT])
        ro = sb("ro", [1, RT])

        hps = [psum(f"hps{i}", [P, 2, BLOCK]) for i in range(3)]
        yps = [psum(f"yps{i}", [P, 4, P]) for i in range(2)]
        tps = psum("tps", [P, 8, P], BF16)
        c0 = psum("c0", [P, TILES, P])
        c1 = psum("c1", [P, TILES, P])

        xload = [sem(f"xload{i}") for i in range(groups)]
        wload = [sem(f"wload{i}") for i in range(2)]
        w_split = sem("w_split")
        aload = sem("aload")
        b2_split, b2_moved = sem("b2_split"), sem("b2_moved")
        const_ready, pool_order = sem("const_ready"), sem("pool_order")
        wT_ready, wT_sb = sem("wT_ready"), sem("wT_sb")
        zero_ready = sem("zero_ready")
        block_in = [sem(f"block_in{i}") for i in range(STEPS)]
        turned, xT_ready = sem("turned"), sem("xT_ready")
        up_done, gelu_done = sem("up_done"), sem("gelu_done")
        hi0_done, hi1_done, lo_done = sem("hi0_done"), sem("hi1_done"), sem("lo_done")
        down_done, y_ready = sem("down_done"), sem("y_ready")
        y_stored = [sem(f"y_stored{i}") for i in range(STEPS)]
        dve_order = sem("dve_order")
        var_ready, rstd_ready, xn_ready = sem("var_ready"), sem("rstd_ready"), sem("xn_ready")
        xn_turned, xnT_ready = sem("xn_turned"), sem("xnT_ready")
        split_hi, split_lo = sem("split_hi"), sem("split_lo")
        gate_done, assign_ready, rank_done = sem("gate_done"), sem("assign_ready"), sem("rank_done")
        dlog_ready, edl_ready, idx_ready, wts_ready = sem("dlog_ready"), sem("edl_ready"), sem("idx_ready"), sem("wts_ready")
        scattered, shared_stored = sem("scattered"), sem("shared_stored")
        sums_ready, count_done, table_ready, padded = sem("sums_ready"), sem("count_done"), sem("table_ready"), sem("padded")
        gidx_ready, gathered, shared_back, combined = sem("gidx_ready"), sem("gathered"), sem("shared_back"), sem("combined")
        gram_done, gram_sb, a_done, a_sb = sem("gram_done"), sem("gram_sb"), sem("a_done"), sem("a_sb")
        scores_done, hd_ready, exp_ready, prob_ready = sem("scores_done"), sem("hd_ready"), sem("exp_ready"), sem("prob_ready")
        ct_done, ct_sb, weff_done, weff_sb, att_done = sem("ct_done"), sem("ct_sb"), sem("weff_done"), sem("weff_sb"), sem("att_done")
        stored, passed = sem("stored"), sem("passed")

        x_v = x.rearrange("(c b) (p j) d -> c p b j d", b=2, j=2)
        out_v = out.rearrange("(c b) (p j) d -> c p b j d", b=2, j=2)

        def norm_count(L, s, which):
            if L < 2:
                return s + L * per_group
            return s * 2 + (2 * per_group + (L - 2) * 2 * per_group + which)

        def expand(ap, shape):
            return ap.to_broadcast(shape)

        def wait_apart(eng, sem, value):
            eng.wait_ge(sem, value)
            eng.sem_inc(passed, 1)

        block = ctx.enter_context(nc.Block())

        @block.sync
        def _(sp):
            for t in range(STEPS):
                sp.sem_inc(y_stored[t], 16)
            sp.sem_inc(shared_stored, 16)
            for g in range(groups):
                for c in range(g * per_group, (g + 1) * per_group):
                    sp.dma_start(X[:, c * TILES:(c + 1) * TILES, :].rearrange("p (b j) d -> p b j d", b=2),
                                 x_v[c]).then_inc(xload[g], 16)
                if g == 0:
                    for n, w in enumerate((wq, wk, wv, wo)):
                        sp.dma_start(watt[:, n, :], w).then_inc(aload, 16)
                    sp.dma_start(gw[:, :], gate_w).then_inc(aload, 16)
                    sp.dma_start(gb[:, :], gate_b.rearrange("(a e) -> a e", a=1).to_broadcast([P, experts])).then_inc(aload, 16)
                    sp.dma_start(b1row[0:experts * HC, :], b1.rearrange("e (j p) -> (e j) p", p=P)).then_inc(aload, 16)
                    sp.dma_start(b1row[experts * HC:NX * HC, :], bs1.rearrange("(j p) -> j p", p=P)).then_inc(aload, 16)
                    sp.dma_start(b2f[:, 0, 0:experts * P], b2.rearrange("(a e) d -> a (e d)", a=1)).then_inc(aload, 16)
                    sp.dma_start(b2f[:, 0, experts * P:], bs2.rearrange("(a d) -> a d", a=1)).then_inc(aload, 16)
                    for n, e in enumerate([SH, *range(experts)]):
                        if n >= 2:
                            sp.wait_ge(w_split, 4 * (n - 1))
                        sp.dma_start(wst[:, n % 2, 0, :], ws1 if e == SH else w1[e]).then_inc(wload[n % 2], 16)
                        sp.dma_start(wst[:, n % 2, 1, :].rearrange("p (j d) -> p j d", j=HC),
                                     (ws2 if e == SH else w2[e]).rearrange("(j p) d -> p j d", p=P)).then_inc(wload[n % 2], 16)
            sp.wait_ge(b2_split, 5)
            sp.wait_ge(const_ready, 2)
            for n in range(3):
                sp.dma_start(b2p[n:n + 1, :], b2s[:, n, :]).then_inc(b2_moved, 16)
            sp.wait_ge(const_ready, 1)
            for g in range(1, 4):
                sp.dma_start(xbuf[g * NR + DUMMY:g * NR + DUMMY + BLOCK, :].rearrange("(p j) d -> p j d", j=2),
                             zero[:, :, :]).then_inc(zero_ready, 16)

            def store_shared(L, s):
                r = s + L * per_group
                wait_apart(sp, split_lo, r + 1)
                row = s * CHUNK + ((L * NR) + SROW)
                sp.dma_start(xbuf[bass.ds(row, CHUNK), :].rearrange("(p t) d -> p t d", t=TILES),
                             xhl[:, :, :]).then_inc(shared_stored, 16)

            def load_block(n, slot, it):
                if not isinstance(n, int):
                    wait_apart(sp, turned, n + (FREE - STEPS + 1))
                row = sp.value_load(rtab[0:1, bass.ds(n, 1)], min_val=0, max_val=4 * NR - BLOCK)
                sp.dma_start(xin[:, slot, :, :], xbuf[bass.ds(row, BLOCK), :].rearrange("(p j) d -> p j d", j=2))\
                    .then_inc(block_in[slot], 16)

            def store_block(L, n, slot):
                wait_apart(sp, y_ready, n + (1 + FREE))
                row = n * BLOCK + (-(L - 1) * NB * BLOCK)
                sp.dma_start(ybuf[(L - 1) % groups][bass.ds(row, BLOCK), :].rearrange("(p j) d -> p j d", j=2), yout[:, slot, :, :])\
                    .then_inc(y_stored[slot], 16)

            def pad_slots(L):
                sp.wait_ge(table_ready, L + 1)
                for e in range(experts):
                    row = sp.value_load(padrow[0:1, e:e + 1], min_val=0, max_val=4 * NR - BLOCK)
                    sp.dma_start(xbuf[bass.ds(row, BLOCK), :].rearrange("(p j) d -> p j d", j=2), zero[:, :, :])\
                        .then_inc(padded, 16)

            def fetch_shared(L, s):
                k = s + (L - 2) * per_group
                wait_apart(sp, combined, k + FREE)
                row = s * CHUNK
                sp.dma_start(ysh[:, :, :], ybuf[L % groups][bass.ds(row, CHUNK), :].rearrange("(p t) d -> p t d", t=TILES))\
                    .then_inc(shared_back, 16)

            def store_chunk(L, s):
                k = s + (L - 2) * per_group
                c = s + (L % groups) * per_group
                wait_apart(sp, combined, k + (FREE + 1))
                for b in range(2):
                    src = X[:, bass.ds(c * TILES + 2 * b, 2), :]
                    dst = out[bass.ds(c * 2 + b, 1)].rearrange("a (p j) d -> (a p) j d", j=2)
                    sp.dma_start(dst, src).then_inc(stored, 16)

            with sp.Fori(0, per_group) as s:
                store_shared(0, s)
            sp.wait_ge(zero_ready, 48)
            sp.wait_ge(scattered, 16)
            sp.wait_ge(shared_stored, 16 * (per_group + 1))
            sp.wait_ge(const_ready, 2)
            sp.sem_inc(turned, FREE)
            for n in range(AHEAD):
                load_block(n, n, 0)
            for L in range(1, 6):
                if L < 5:
                    pad_slots(L - 1)
                    sp.wait_ge(scattered, 128 * per_group * L + 16)
                    sp.wait_ge(padded, 16 * experts * L)
                if L >= 2:
                    for t in range(STEPS):
                        sp.wait_ge(y_stored[t], 16 * (per_group * (L - 1) + 1))
                with sp.Fori(0, per_group) as s:
                    if L < 4:
                        wait_apart(sp, shared_stored, s * 16 + (16 * (per_group * L + 1)))
                    if L >= 2:
                        fetch_shared(L, s)
                    if L < 5:
                        for u in range(STEPS):
                            n = s * STEPS + ((L - 1) * NB + u)
                            load_block(n + AHEAD, (u + AHEAD) % STEPS, None)
                            store_block(L, n, u)
                    if L < 4:
                        store_shared(L, s)
                    if L >= 4:
                        store_chunk(L, s)
            sp.wait_ge(stored, 16 * 2 * chunks)
            for t in range(STEPS):
                sp.wait_ge(y_stored[t], 16 * (per_group * 4 + 1))
            for t in range(AHEAD):
                sp.wait_ge(block_in[t], 16 * (4 * per_group + 1))

        @block.gpsimd
        def _(pool):
            pool.memset(zero[:, :, :], 0.0).then_inc(const_ready, 1)
            order = [0]

            def put(inst):
                order[0] += 1
                inst.then_inc(pool_order, 1)
            put(pool.memset(etab[:, :], SH))
            put(pool.memset(idf[:, :], 0.0))
            put(pool.memset(idb[:, :], 0.0))
            put(pool.memset(onesb[:, :], 1.0))
            put(pool.memset(upper[:, :], 0.0))
            put(pool.memset(sel3[:, :], 1.0))
            put(pool.memset(mask[:, :], 1.0))
            put(pool.memset(tri[:, :, :], 1.0))
            put(pool.memset(mhalf[:, :], -0.5))
            put(pool.memset(ebase[:, :], E_BASE))
            put(pool.memset(expbase[:, :], EXP_BASE))
            put(pool.memset(b2p[:, :], 0.0))
            put(pool.memset(asum[:, :], 0.0))
            put(pool.memset(rtab[:, :], DUMMY))
            put(pool.iota(rev[:, :], [[-1, experts]], base=experts, channel_multiplier=0, allow_small_or_imprecise_dtypes=True))
            put(pool.iota(ecap[:, :], [[CAP, experts]], base=0, channel_multiplier=0, allow_small_or_imprecise_dtypes=True))
            put(pool.iota(nidx[:, :], [[1, RT]], base=0, channel_multiplier=0, allow_small_or_imprecise_dtypes=True))
            pool.wait_ge(pool_order, order[0])
            for g in range(4):
                put(pool.iota(rtab[:, g * NB:g * NB + SHARED], [[BLOCK, SHARED]], base=g * NR + SROW, channel_multiplier=0))
            for m in (idf, idb):
                put(pool.affine_select(out=m[:, :], in_=m[:, :], compare_op=ALU.not_equal, fill=1.0, base=0,
                                       pattern=[[-1, P]], channel_multiplier=1))
            put(pool.affine_select(out=upper[:, :], in_=upper[:, :], compare_op=ALU.is_ge, fill=1.0, base=0,
                                   pattern=[[-1, P]], channel_multiplier=1))
            put(pool.affine_select(out=sel3[:, :], in_=sel3[:, :], compare_op=ALU.is_ge, fill=0.0, base=2,
                                   pattern=[[0, P]], channel_multiplier=-1))
            put(pool.affine_select(out=tri[:, :, :], in_=tri[:, :, :], compare_op=ALU.is_ge, fill=0.0, base=0,
                                   pattern=[[1, experts], [-1, experts]], channel_multiplier=0))
            mk = mask[:, :].rearrange("p (k i) -> p k i", i=HEAD)
            put(pool.affine_select(out=mk, in_=mk, compare_op=ALU.is_ge, fill=0.0, base=0,
                                   pattern=[[-HEAD, P // HEAD], [0, HEAD]], channel_multiplier=1))
            pool.wait_ge(pool_order, order[0])
            pool.affine_select(out=mk, in_=mk, compare_op=ALU.is_ge, fill=0.0, base=HEAD - 1,
                               pattern=[[HEAD, P // HEAD], [0, HEAD]], channel_multiplier=-1).then_inc(const_ready, 1)
            pool.dma_start(xbuf[DUMMY:DUMMY + BLOCK, :].rearrange("(p j) d -> p j d", j=2), zero[:, :, :]).then_inc(scattered, 16)
            pool.sem_inc(combined, FREE)

            def root(n):
                pool.wait_ge(var_ready, n + 1)
                pool.tensor_tensor(rstd[:, :], ve[:, :], mhalf[:, :], ALU.pow).then_inc(rstd_ready, 1)

            def gate_exp(r):
                pool.wait_ge(dlog_ready, r + 1)
                pool.tensor_tensor(edl[:, :], ebase[:, :], dlog[:, :], ALU.pow).then_inc(edl_ready, 1)

            def head_exp(t):
                pool.wait_ge(hd_ready, t + 1)
                pool.tensor_tensor(hex_[:, :, :], expbase[:, :].rearrange("p (b i) -> p b i", b=2), hd2[:, :, :], ALU.pow)\
                    .then_inc(exp_ready, 1)

            def scatter(L, s):
                r = s + L * per_group
                c = s + (L % groups) * per_group
                pool.wait_ge(split_lo, r + 1)
                wait_apart(pool, idx_ready, r + 1)
                for a in range(2 * TILES):
                    pool.indirect_dma_start(xbuf[:, :], bass.IndirectOffsetOnAxis(idx[:, a:a + 1], 0),
                                            xhl[:, a % TILES, :], None).then_inc(scattered, 16)

            def gather(L, s):
                k = s + (L - 2) * per_group
                c = s + (L % groups) * per_group
                pool.wait_ge(combined, k + FREE)
                if not isinstance(k, int) or k > 0:
                    pool.wait_ge(gathered, k * 128)
                pool.wait_ge(table_ready, L - 1)
                pool.tensor_copy(gidx[:, :], gix[:, bass.ds(c, 1), :].rearrange("p a k -> p (a k)")).then_inc(gidx_ready, 1)
                wait_apart(pool, gidx_ready, k + 1)
                for a in range(2 * TILES):
                    pool.indirect_dma_start(yg[:, a, :], None, ybuf[L % groups][:, :],
                                            bass.IndirectOffsetOnAxis(gidx[:, a:a + 1], 0)).then_inc(gathered, 16)

            for L in range(2):
                with pool.Fori(0, per_group) as s:
                    root(norm_count(L, s, 1))
                    gate_exp(s + L * per_group)
                    scatter(L, s)
            for L in range(2, 6):
                for t in range(STEPS):
                    pool.wait_ge(y_stored[t], 16 * (per_group * (L - 1) + 1))
                gather(L, 0)

                def rest(s, last):
                    if L < 4:
                        root(norm_count(L, s, 0))
                        head_exp(s + (L - 2) * per_group)
                        root(norm_count(L, s, 1))
                    if not last:
                        gather(L, s + 1)
                    if L < 4:
                        gate_exp(s + L * per_group)
                        scatter(L, s)
                with pool.Fori(0, per_group - 1) as s:
                    rest(s, False)
                rest(per_group - 1, True)
            pool.wait_ge(scattered, 16 + 128 * per_group * 4)

        @block.tensor
        def _(pe):
            pe.wait_ge(aload, 160)
            pe.wait_ge(const_ready, 2)
            for n, m in enumerate((0, 1, 3)):
                pe.transpose(c0[:, n, :], watt[:, m, :], idf[:, :])
            pe.transpose(c0[:, 3, 0:NX * HC], b1row[:, :], idf[0:NX * HC, 0:NX * HC]).then_inc(wT_ready, 1)
            pe.wait_ge(wT_sb, 4)

            def turn_chunk(n):
                pe.wait_ge(xn_ready, n + 1)
                for t in range(TILES):
                    last = pe.transpose(c0[:, t, :], xn[:, t, :], idf[:, :])
                last.then_inc(xn_turned, 1)

            def gate(n, r):
                pe.wait_ge(xnT_ready, n + 1)
                for t in range(TILES):
                    last = pe.matmul(c1[:, 0, t * experts:(t + 1) * experts], xnT[:, t * P:(t + 1) * P], gw[:, :],
                                     start=True, stop=True)
                last.then_inc(gate_done, 1)

            def rank(r):
                pe.wait_ge(assign_ready, r + 1)
                o = c1[:, 0, 0:TILES * experts].rearrange("p (t e) -> p t e", t=TILES)
                pe.matmul(o, upper[:, :], assign[:, :, :], start=True, stop=False)
                pe.matmul(o, onesb[:, :], asum[:, :].unsqueeze(1).to_broadcast([P, TILES, experts]), start=False, stop=False)
                for t in range(1, TILES):
                    last = pe.matmul(o[:, t:, :], onesb[:, :], assign[:, 0:TILES - t, :], start=False, stop=t == TILES - 1)
                last.then_inc(rank_done, 1)

            def count(L):
                pe.wait_ge(sums_ready, L + 1)
                pe.matmul(c1[:, 0, 0:experts], onesb[:, :], asum[:, :], start=True, stop=True).then_inc(count_done, 1)

            def att_gram(n, t):
                pe.wait_ge(xn_ready, n + 1)
                for b in range(2):
                    for j in range(2):
                        v = xn[:, 2 * b + j, :]
                        last = pe.matmul(c1[:, b, :], v, v, start=j == 0, stop=j == 1)
                last.then_inc(gram_done, 1)
                turn_chunk(n)

            def att_a(t):
                pe.wait_ge(gram_sb, t + 1)
                for b in range(2):
                    last = pe.matmul(c1[:, b, :], gram[:, b, :], wkT[:, :], start=True, stop=True)
                last.then_inc(a_done, 1)

            def att_scores(t):
                pe.wait_ge(a_sb, t + 1)
                for b in range(2):
                    last = pe.matmul(c1[:, b, :], gA[:, b, :], wqT[:, :], start=True, stop=True)
                last.then_inc(scores_done, 1)

            def att_ct(t):
                pe.wait_ge(prob_ready, t + 1)
                for b in range(2):
                    last = pe.matmul(c1[:, b, :], prob[:, b, :], watt[:, 2, :], start=True, stop=True)
                last.then_inc(ct_done, 1)

            def att_weff(t):
                pe.wait_ge(ct_sb, t + 1)
                for b in range(2):
                    last = pe.matmul(c1[:, b, :], cT[:, b, :], woT[:, :], start=True, stop=True)
                last.then_inc(weff_done, 1)

            def att_out(n, t):
                pe.wait_ge(weff_sb, t + 1)
                pe.wait_ge(xnT_ready, n + 1)
                for a in range(TILES):
                    last = pe.matmul(c0[:, a, :], xnT[:, a * P:(a + 1) * P], weff[:, a // 2, :], start=True, stop=True)
                last.then_inc(att_done, 1)

            def turn_block(n, slot, landed):
                pe.wait_ge(block_in[slot], landed)
                pe.wait_ge(xT_ready, n + FREE)
                for h in range(2):
                    for j in range(2):
                        last = pe.transpose(tps[:, 2 * h + j, :], xin[:, slot, j, h * P:(h + 1) * P], idb[:, :])
                last.then_inc(turned, 1)

            def up(n, slot, e):
                pe.wait_ge(xT_ready, n + FREE + 1)
                for q in range(2):
                    at = 2 * slot + q
                    bank = hps[HBANK[at]]
                    pe.wait_ge(gelu_done, n * 2 + (q + 1 - back(HBANK, at) + FREE))
                    for jj in range(2):
                        j = 2 * q + jj
                        wh = w1h[:, bass.ds(e, 1), j * P:(j + 1) * P].rearrange("p a d -> p (a d)")
                        wl = w1l[:, bass.ds(e, 1), j * P:(j + 1) * P].rearrange("p a d -> p (a d)")
                        pe.matmul(bank[:, jj, :], wh, xT[:, slot, 0, :], start=True, stop=False)
                        pe.matmul(bank[:, jj, :], wh, xT[:, slot, 1, :], start=False, stop=False)
                        last = pe.matmul(bank[:, jj, :], wl, xT[:, slot, 0, :], start=False, stop=True)
                    last.then_inc(up_done, 1)

            def down(n, slot, e):
                g = GELU_SLOT[slot]
                bank = yps[YBANK[slot]]
                pe.wait_ge(y_ready, n + (1 - back(YBANK, slot) + FREE))
                bias = b2p[:, bass.ds(e * P, P)].unsqueeze(1).to_broadcast([P, 2, P])
                pe.matmul(bank[:, 0:2, :], sel3[:, :], bias, start=True, stop=False, skip_group_check=True)
                for q in range(2):
                    pe.wait_ge(lo_done, n * 2 + (q + 1))
                    if q == 0:
                        pe.wait_ge(hi0_done, n + 1)
                    else:
                        pe.wait_ge(hi1_done, n + 1)
                    for t in range(2):
                        for j in (2 * q, 2 * q + 1):
                            wh = w2h[:, bass.ds(e, 1), j * P:(j + 1) * P].rearrange("p a d -> p (a d)")
                            wl = w2l[:, bass.ds(e, 1), j * P:(j + 1) * P].rearrange("p a d -> p (a d)")
                            hi, lo = gh[:, g, j, t * P:(t + 1) * P], gl[:, g, j, t * P:(t + 1) * P]
                            pe.matmul(bank[:, t, :], hi, wh, start=False, stop=False, skip_group_check=True)
                            pe.matmul(bank[:, t, :], hi, wl, start=False, stop=False, skip_group_check=True)
                            last = pe.matmul(bank[:, t, :], lo, wh, start=False, stop=q == 1 and j == HC - 1,
                                             skip_group_check=True)
                last.then_inc(down_done, 1)

            def expert(n):
                return pe.value_load(etab[0:1, bass.ds(n, 1)], min_val=0, max_val=SH)

            pe.sem_inc(down_done, FREE)
            for s_ in range(1):
                with pe.Fori(0, per_group) as s:
                    turn_chunk(norm_count(0, s, 1))
                    gate(norm_count(0, s, 1), s)
                    rank(s)
            count(0)
            pe.wait_ge(w_split, 4 * NX)
            pe.wait_ge(b2_moved, 48)
            turn_block(0, 0, 16)
            up(0, 0, SH)
            turn_block(1, 1, 16)
            for L in range(1, 5):
                if 1 <= L <= 4:
                    pe.wait_ge(table_ready, L)
                with pe.Fori(0, per_group) as s:
                    n0 = norm_count(L, s, 0)
                    n1 = norm_count(L, s, 1)
                    t_ = s + (L - 2) * per_group
                    r_ = s + L * per_group
                    pieces = {}
                    if L == 1:
                        pieces = {4: lambda: turn_chunk(n1), 6: lambda: gate(n1, r_), 8: lambda: rank(r_)}
                    elif L < 4:
                        pieces = {2: lambda: att_gram(n0, t_), 3: lambda: att_a(t_), 4: lambda: att_scores(t_),
                                  7: lambda: att_ct(t_), 8: lambda: att_weff(t_), 9: lambda: att_out(n0, t_),
                                  11: lambda: turn_chunk(n1), 12: lambda: gate(n1, r_), 13: lambda: rank(r_)}
                    if L < 5:
                        for u in range(STEPS):
                            n = s * STEPS + ((L - 1) * NB + u)
                            it = s + (L - 1) * per_group
                            slot2 = (u + 2) % STEPS
                            turn_block(n + 2, slot2, it * 16 + (16 * (1 + (u + 2) // STEPS)))
                            up(n + 1, (u + 1) % STEPS, expert(n + 1))
                            if 2 * u in pieces:
                                pieces[2 * u]()
                            down(n, u, expert(n))
                            if 2 * u + 1 in pieces:
                                pieces[2 * u + 1]()
                if L < 4:
                    count(L)

        @block.scalar
        def _(act):
            act.wait_ge(wT_ready, 1)
            for n, m in enumerate((wqT, wkT, woT)):
                act.activation(m[:, :], c0[:, n, :], ACT.Copy).then_inc(wT_sb, 1)
            act.activation(b1t[:, :], c0[:, 3, 0:NX * HC], ACT.Copy).then_inc(wT_sb, 1)

            def split_high(L, s):
                r = s + L * per_group
                act.wait_ge(xn_ready, norm_count(L, s, 1) + 1)
                act.wait_ge(scattered, r * 128 + 16)
                act.wait_ge(shared_stored, r * 16 + 16)
                act.activation(xhl[:, :, 0:P], xn[:, :, :], ACT.Copy).then_inc(split_hi, 1)

            def take_xnT(n):
                act.wait_ge(xn_turned, n + 1 + 1)
                act.activation(xnT[:, :], c0[:, :, :].rearrange("p t d -> p (t d)"), ACT.Copy).then_inc(xnT_ready, 1)

            def take(done, t, dst, kept):
                act.wait_ge(done, t + 1)
                act.activation(dst[:, :, :], c1[:, 0:2, :], ACT.Copy).then_inc(kept, 1)

            def gelu_pair(n, slot, q, e):
                g = GELU_SLOT[slot]
                at = 2 * slot + q
                act.wait_ge(up_done, n * 2 + (q + 1))
                if q == 0:
                    act.wait_ge(down_done, n + (1 - back(GELU_SLOT, slot) + FREE))
                for jj in range(2):
                    j = 2 * q + jj
                    last = act.activation(g32[:, g, j, :], hps[HBANK[at]][:, jj, :], ACT.Gelu,
                                          bias=b1t[:, bass.ds(e * HC + j, 1)])
                last.then_inc(gelu_done, 1)

            def high0(n, slot):
                g = GELU_SLOT[slot]
                act.wait_ge(gelu_done, n * 2 + (1 + FREE))
                act.activation(gh[:, g, 0:2, :], g32[:, g, 0:2, :], ACT.Copy).then_inc(hi0_done, 1)

            def leave(n, slot, it):
                act.wait_ge(down_done, n + (1 + FREE))
                act.wait_ge(y_stored[slot], it * 16 + 16)
                act.activation(yout[:, slot, :, :], yps[YBANK[slot]][:, 0:2, :], ACT.Copy).then_inc(y_ready, 1)

            def expert(n):
                return act.value_load(etab[0:1, bass.ds(n, 1)], min_val=0, max_val=SH)

            act.sem_inc(xn_turned, 1)
            act.sem_inc(gelu_done, FREE)
            act.sem_inc(y_ready, FREE)
            with act.Fori(0, per_group) as s:
                split_high(0, s)
                take_xnT(norm_count(0, s, 1))
            act.wait_ge(const_ready, 2)
            gelu_pair(0, 0, 0, SH)
            high0(0, 0)
            gelu_pair(0, 0, 1, SH)
            for L in range(1, 5):
                act.wait_ge(table_ready, L)
                with act.Fori(0, per_group) as s:
                    n0 = norm_count(L, s, 0)
                    n1 = norm_count(L, s, 1)
                    t_ = s + (L - 2) * per_group
                    pieces = {}
                    if L == 1:
                        pieces = {4: lambda: (split_high(L, s), take_xnT(n1))}
                    elif L < 4:
                        pieces = {2: lambda: take(gram_done, t_, gram, gram_sb),
                                  3: lambda: (take(a_done, t_, gA, a_sb), take_xnT(n0)),
                                  7: lambda: take(ct_done, t_, cT, ct_sb),
                                  8: lambda: take(weff_done, t_, weff, weff_sb),
                                  11: lambda: (split_high(L, s), take_xnT(n1))}
                    for u in range(STEPS):
                        n = s * STEPS + ((L - 1) * NB + u)
                        it = s + (L - 1) * per_group
                        e = expert(n + 1)
                        up_slot = (u + 1) % STEPS
                        gelu_pair(n + 1, up_slot, 0, e)
                        high0(n + 1, up_slot)
                        gelu_pair(n + 1, up_slot, 1, e)
                        if 2 * u in pieces:
                            pieces[2 * u]()
                        leave(n, u, it)
                        if 2 * u + 1 in pieces:
                            pieces[2 * u + 1]()

        @block.vector
        def _(dve):
            class Order:
                base, n = 0, 0

            def step(inst):
                Order.n += 1
                inst.then_inc(dve_order, 1)

            def settle():
                dve.wait_ge(dve_order, Order.base + Order.n)

            for n, e in enumerate([SH, *range(experts)]):
                dve.wait_ge(wload[n % 2], 32 * (n // 2 + 1))
                for k, (wh, wl) in enumerate(((w1h, w1l), (w2h, w2l))):
                    dve.tensor_copy(wh[:, e, :], wst[:, n % 2, k, :]).then_inc(w_split, 1)
                    dve.wait_ge(w_split, 4 * n + 2 * k + 1)
                    dve.tensor_tensor(wl[:, e, :], wst[:, n % 2, k, :], wh[:, e, :], ALU.subtract).then_inc(w_split, 1)
            dve.wait_ge(aload, 160)
            dve.tensor_copy(b2s[:, 0, :], b2f[:, 0, :]).then_inc(b2_split, 1)
            dve.wait_ge(b2_split, 1)
            dve.tensor_tensor(b2f[:, 1, :], b2f[:, 0, :], b2s[:, 0, :], ALU.subtract).then_inc(b2_split, 1)
            dve.wait_ge(b2_split, 2)
            dve.tensor_copy(b2s[:, 1, :], b2f[:, 1, :]).then_inc(b2_split, 1)
            dve.wait_ge(b2_split, 3)
            dve.tensor_tensor(b2f[:, 2, :], b2f[:, 1, :], b2s[:, 1, :], ALU.subtract).then_inc(b2_split, 1)
            dve.wait_ge(b2_split, 4)
            dve.tensor_copy(b2s[:, 2, :], b2f[:, 2, :]).then_inc(b2_split, 1)
            dve.wait_ge(const_ready, 2)

            def stats(c, n):
                for t in range(TILES):
                    step(dve.bn_stats(st6[:, t, :], X[:, bass.ds(c * TILES + t, 1), :].rearrange("p a d -> p (a d)")))
                wait_apart(dve, dve_order, Order.base + Order.n)
                for t in range(TILES):
                    step(dve.bn_aggr(mv[:, t, :], st6[:, t, :]))
                settle()
                dve.tensor_scalar(ve[:, :], mv[:, :, 1], EPS, None, ALU.add).then_inc(var_ready, 1)

            def normalise(c, n):
                dve.wait_ge(rstd_ready, n + 1)
                dve.wait_ge(xn_turned, n + 1)
                for t in range(TILES):
                    last = dve.tensor_scalar(xn[:, t, :], X[:, bass.ds(c * TILES + t, 1), :].rearrange("p a d -> p (a d)"),
                                             mv[:, t, 0:1], rstd[:, t:t + 1], ALU.subtract, ALU.mult)
                last.then_inc(xn_ready, 1)

            def split_low(L, s):
                r = s + L * per_group
                dve.wait_ge(split_hi, r + 1)
                dve.tensor_tensor(xhl[:, :, P:2 * P], xn[:, :, :], xhl[:, :, 0:P], ALU.subtract).then_inc(split_lo, 1)

            def over_e(ap):
                return ap.unsqueeze(2).to_broadcast([P, TILES, experts])

            def over_t(ap):
                return ap.unsqueeze(1).to_broadcast([P, TILES, experts])

            def choose(L, r, k, src):
                step(dve.reduce_max(m12[:, k, :], src, AX.X))
                settle()
                step(dve.tensor_tensor(cand[:, :, :], src, over_e(m12[:, k, :]), ALU.is_ge))
                settle()
                step(dve.tensor_tensor(cand[:, :, :], cand[:, :, :], over_t(rev[:, :]), ALU.mult))
                settle()
                step(dve.reduce_max(first[:, :], cand[:, :, :], AX.X))
                settle()
                step(dve.tensor_tensor(oh[:, k, :, :], over_t(rev[:, :]), over_e(first[:, :]), ALU.is_equal))
                settle()

            def route(L, s):
                r = s + L * per_group
                dve.wait_ge(gate_done, r + 1)
                step(dve.tensor_tensor(lg[:, :, :], c1[:, 0, 0:TILES * experts].rearrange("p (t e) -> p t e", t=TILES),
                                       over_t(gb[:, :]), ALU.add))
                settle()
                choose(L, r, 0, lg[:, :, :])
                step(dve.scalar_tensor_tensor(lg2[:, :, :], oh[:, 0, :, :], -BIG, lg[:, :, :], ALU.mult, ALU.add))
                settle()
                choose(L, r, 1, lg2[:, :, :])
                dve.tensor_tensor(dlog[:, :], m12[:, 1, :], m12[:, 0, :], ALU.subtract).then_inc(dlog_ready, 1)
                dve.tensor_tensor(assign[:, :, :], oh[:, 0, :, :], oh[:, 1, :, :], ALU.add).then_inc(assign_ready, 1)

            def slots(L, s):
                r = s + L * per_group
                dve.wait_ge(rank_done, r + 1)
                dve.wait_ge(scattered, r * 128 + 16)
                step(dve.tensor_tensor(rk[:, :, :], c1[:, 0, 0:TILES * experts].rearrange("p (t e) -> p t e", t=TILES),
                                       over_t(ecap[:, :]), ALU.add))
                dve.wait_ge(assign_ready, r + 1)
                step(dve.reduce_sum(arow[:, :], assign[:, :, :].rearrange("p t e -> p e t"), AX.X))
                settle()
                step(dve.tensor_tensor(pick[:, :, :, :], oh[:, :, :, :],
                                       rk[:, :, :].unsqueeze(1).to_broadcast([P, 2, TILES, experts]), ALU.mult))
                step(dve.tensor_tensor(asum[:, :], asum[:, :], arow[:, :], ALU.add))
                settle()
                here = pos[:, bass.ds(s, 1), :]
                step(dve.reduce_sum(here.rearrange("p a (k t) -> p (a k) t", k=2), pick[:, :, :, :], AX.X))
                settle()
                dve.tensor_scalar(idx[:, :], here.rearrange("p a k -> p (a k)"), float(L * NR), None, ALU.add).then_inc(idx_ready, 1)

            def weights(L, s):
                r = s + L * per_group
                c = s + (L % groups) * per_group
                dve.wait_ge(edl_ready, r + 1)
                step(dve.tensor_scalar(den[:, :], edl[:, :], 1.0, None, ALU.add))
                settle()
                step(dve.reciprocal(rden[:, :], den[:, :]))
                settle()
                w = [wts[:, k, bass.ds(c * TILES, TILES)] for k in range(2)]
                step(dve.tensor_scalar(w[0], rden[:, :], 0.5, None, ALU.mult))
                dve.scalar_tensor_tensor(w[1], edl[:, :], 0.5, rden[:, :], ALU.mult, ALU.mult).then_inc(wts_ready, 1)

            ROUTE_STEPS = 8 + 12 + 5 + 3
            COMBINE_STEPS = 4 + 4
            ATT_STEPS = 8 + 6 + 1

            def table(L):
                def bc(ap, n):
                    return ap.unsqueeze(1).to_broadcast([ap.shape[0], n, experts])
                dve.wait_ge(count_done, L + 1)
                step(dve.tensor_copy(cnt[:, :], c1[:, 0, 0:experts]))
                step(dve.memset(asum[:, :], 0.0))
                settle()
                step(dve.tensor_scalar(cnt_i[:, :], cnt[:, :], float(BLOCK - 1), None, ALU.add))
                step(dve.tensor_tensor(padf[:, :], cnt[0:1, :], ecap[0:1, :], ALU.add))
                settle()
                step(dve.tensor_scalar(padrow[:, :], padf[:, :], float(L * NR), None, ALU.add))
                step(dve.tensor_scalar(nb_i[:, :], cnt_i[:, :], BLOCK.bit_length() - 1, None, ALU.arith_shift_right))
                settle()
                step(dve.tensor_copy(nb[:, :], nb_i[:, :]))
                settle()
                step(dve.tensor_tensor(cumm[:, :, :], tri[:, :, :], bc(nb[0:1, :], experts), ALU.mult))
                settle()
                step(dve.reduce_sum(cum[:, :], cumm[:, :, :], AX.X))
                settle()
                step(dve.tensor_tensor(le[:, :, :], bc(cum[:, :], RT), nidx[:, :].unsqueeze(2).to_broadcast([1, RT, experts]),
                                       ALU.is_le))
                settle()
                step(dve.reduce_sum(en[:, :], le[:, :, :], AX.X))
                step(dve.tensor_tensor(le2[:, :, :], le[:, :, :], bc(nb[0:1, :], RT), ALU.mult))
                settle()
                step(dve.reduce_sum(cp[:, :], le2[:, :, :], AX.X))
                step(dve.tensor_scalar(ok[:, :], en[:, :], float(experts), float(BLOCK), ALU.is_lt, ALU.mult))
                settle()
                step(dve.tensor_tensor(bi[:, :], nidx[:, :], cp[:, :], ALU.subtract))
                settle()
                step(dve.tensor_tensor(bo[:, :], bi[:, :], ok[:, :], ALU.mult))
                step(dve.tensor_scalar(ro[:, :], en[:, :], float(CAP), float(L * NR), ALU.mult, ALU.add))
                step(dve.tensor_copy(etab[:, L * NB + SHARED:(L + 1) * NB], en[:, :]))
                settle()
                step(dve.tensor_tensor(rtab[:, L * NB + SHARED:(L + 1) * NB], ro[:, :], bo[:, :], ALU.add))
                step(dve.memset(hop[:, 0:1], float(SHARED * BLOCK)))
                step(dve.tensor_scalar(hop[:, 1:experts], nb[:, 0:experts - 1], float(BLOCK), -float(CAP), ALU.mult, ALU.add))
                allpos = pos[:, :, :].rearrange("p c k -> p (c k)")
                n = per_group * 2 * TILES
                step(dve.tensor_tensor(posge[:, :, :], allpos.unsqueeze(2).to_broadcast([P, n, experts]), bc(ecap[:, :], n), ALU.is_ge))
                settle()
                step(dve.tensor_tensor(posge[:, :, :], posge[:, :, :], bc(hop[:, :], n), ALU.mult))
                settle()
                step(dve.reduce_sum(shift[:, :], posge[:, :, :], AX.X))
                settle()
                g = L % groups
                dve.tensor_tensor(gix[:, g * per_group:(g + 1) * per_group, :].rearrange("p c k -> p (c k)"), allpos, shift[:, :],
                                  ALU.add).then_inc(table_ready, 1)

            TABLE_STEPS = 24

            def note_sums():
                settle()
                dve.tensor_copy(arow[:, 0:1], asum[:, 0:1]).then_inc(sums_ready, 1)

            def combine(L, s):
                k = s + (L - 2) * per_group
                c = s + (L % groups) * per_group
                dve.wait_ge(gathered, k * 128 + 128)
                dve.wait_ge(shared_back, k * 16 + 16)
                xc = [X[:, bass.ds(c * TILES + t, 1), :].rearrange("p a d -> p (a d)") for t in range(TILES)]
                for ch in range(2):
                    for t in range(TILES):
                        step(dve.scalar_tensor_tensor(xc[t], yg[:, ch * TILES + t, :], wts[:, ch, bass.ds(c * TILES + t, 1)],
                                                      xc[t], ALU.mult, ALU.add))
                    settle()
                xa = X[:, bass.ds(c * TILES, TILES), :]
                dve.scalar_tensor_tensor(xa, ysh[:, :, :], 0.5, xa, ALU.mult, ALU.add).then_inc(combined, 1)
                wait_apart(dve, combined, k + (1 + FREE))

            def att_soft1(t):
                dve.wait_ge(scores_done, t + 1)
                step(dve.tensor_tensor(gm[:, :, :], c1[:, 0:2, :], mask[:, :].unsqueeze(1).to_broadcast([P, 2, P]), ALU.mult))
                settle()
                step(dve.reduce_sum(hd[:, :, :], gm[:, :, :].rearrange("p b (k i) -> p b i k", i=HEAD), AX.X))
                settle()
                step(dve.reduce_max(hmx[:, :], hd[:, :, :], AX.X))
                settle()
                dve.tensor_tensor(hd2[:, :, :], hd[:, :, :], hmx[:, :].unsqueeze(2).to_broadcast([P, 2, HEAD]), ALU.subtract)\
                    .then_inc(hd_ready, 1)

            def att_soft2(t):
                dve.wait_ge(exp_ready, t + 1)
                step(dve.reduce_sum(hsum[:, :], hex_[:, :, :], AX.X))
                settle()
                step(dve.reciprocal(hrec[:, :], hsum[:, :]))
                settle()
                step(dve.tensor_tensor(hp[:, :, :], hex_[:, :, :], hrec[:, :].unsqueeze(2).to_broadcast([P, 2, HEAD]), ALU.mult))
                settle()
                for b in range(2):
                    last = dve.tensor_tensor(prob[:, b, :].rearrange("p (k i) -> p k i", i=HEAD),
                                             mask[:, :].rearrange("p (k i) -> p k i", i=HEAD),
                                             hp[:, b, :].unsqueeze(1).to_broadcast([P, P // HEAD, HEAD]), ALU.mult)
                last.then_inc(prob_ready, 1)

            def att_add(L, s, t):
                c = s + (L % groups) * per_group
                dve.wait_ge(att_done, t + 1)
                xa = X[:, bass.ds(c * TILES, TILES), :]
                step(dve.tensor_tensor(xa, c0[:, :, :], xa, ALU.add))
                wait_apart(dve, dve_order, Order.base + Order.n)

            def take_xT(n, slot):
                dve.wait_ge(turned, n + (1 + FREE))
                dve.tensor_copy(xT[:, slot, :, :].rearrange("p h s -> p (h s)"),
                                tps[:, 0:4, :].rearrange("p a b -> p (a b)")).then_inc(xT_ready, 1)

            def split_block(n, slot):
                g = GELU_SLOT[slot]
                dve.wait_ge(hi0_done, n + 1)
                dve.tensor_tensor(gl[:, g, 0:2, :], g32[:, g, 0:2, :], gh[:, g, 0:2, :], ALU.subtract).then_inc(lo_done, 1)
                dve.wait_ge(gelu_done, n * 2 + (2 + FREE))
                dve.tensor_copy(gh[:, g, 2:4, :], g32[:, g, 2:4, :]).then_inc(hi1_done, 1)
                dve.wait_ge(hi1_done, n + 1)
                dve.tensor_tensor(gl[:, g, 2:4, :], g32[:, g, 2:4, :], gh[:, g, 2:4, :], ALU.subtract).then_inc(lo_done, 1)

            dve.sem_inc(xT_ready, FREE)
            dve.wait_ge(xload[0], 16 * per_group)
            total = 0
            with dve.Fori(0, per_group) as s:
                Order.base, Order.n = s * ROUTE_STEPS, 0
                n1 = norm_count(0, s, 1)
                stats(s, n1)
                normalise(s, n1)
                split_low(0, s)
                route(0, s)
                slots(0, s)
                weights(0, s)
                assert Order.n == ROUTE_STEPS, Order.n
            total += per_group * ROUTE_STEPS
            Order.base, Order.n = total, 0
            note_sums()
            table(0)
            assert Order.n == TABLE_STEPS, Order.n
            total += TABLE_STEPS
            dve.wait_ge(const_ready, 2)
            take_xT(0, 0)
            split_block(0, 0)
            take_xT(1, 1)
            dve.wait_ge(xload[1], 16 * per_group)
            for L in range(1, 6):
                per = {1: ROUTE_STEPS, 2: ROUTE_STEPS + COMBINE_STEPS + ATT_STEPS, 3: ROUTE_STEPS + COMBINE_STEPS + ATT_STEPS,
                       4: COMBINE_STEPS, 5: COMBINE_STEPS}[L]
                with dve.Fori(0, per_group) as s:
                    Order.base, Order.n = s * per + total, 0
                    n0 = norm_count(L, s, 0)
                    n1 = norm_count(L, s, 1)
                    t_ = s + (L - 2) * per_group
                    c = s + (L % groups) * per_group
                    if L == 1:
                        pieces = {0: lambda: stats(c, n1), 2: lambda: normalise(c, n1), 4: lambda: split_low(L, s),
                                  6: lambda: route(L, s), 8: lambda: slots(L, s), 10: lambda: weights(L, s)}
                    elif L < 4:
                        pieces = {0: lambda: (combine(L, s), stats(c, n0)), 1: lambda: normalise(c, n0),
                                  4: lambda: att_soft1(t_), 6: lambda: att_soft2(t_),
                                  9: lambda: (att_add(L, s, t_), stats(c, n1)), 10: lambda: normalise(c, n1),
                                  11: lambda: split_low(L, s), 12: lambda: route(L, s),
                                  13: lambda: (slots(L, s), weights(L, s))}
                    else:
                        pieces = {6: lambda: combine(L, s)}
                    if L < 5:
                        for u in range(STEPS):
                            n = s * STEPS + ((L - 1) * NB + u)
                            take_xT(n + 2, (u + 2) % STEPS)
                            split_block(n + 1, (u + 1) % STEPS)
                            if 2 * u in pieces:
                                pieces[2 * u]()
                            if 2 * u + 1 in pieces:
                                pieces[2 * u + 1]()
                    else:
                        pieces[6]()
                    assert Order.n == per, (L, Order.n, per)
                total += per_group * per
                if L < 4:
                    Order.base, Order.n = total, 0
                    note_sums()
                    table(L)
                    total += TABLE_STEPS


_INS = ['L0_attn_x', 'L0_attn_Wq', 'L0_attn_Wk', 'L0_attn_Wv', 'L0_attn_Wo', 'L0_ffn_gate_w', 'L0_ffn_gate_b',
        'L0_ffn_w1', 'L0_ffn_b1', 'L0_ffn_w2', 'L0_ffn_b2', 'L0_ffn_ws1', 'L0_ffn_bs1', 'L0_ffn_ws2', 'L0_ffn_bs2']


def kernel(**inputs):
    import numpy as _np
    import concourse.bacc as _bacc
    from concourse import mybir as _mybir
    from concourse.bass_utils import run_bass_kernel_spmd as _run

    nc = _bacc.Bacc("TRN2", target_bir_lowering=False, num_devices=1)
    arrays, args = {}, []
    for name in _INS:
        a = _np.ascontiguousarray(inputs[name])
        arrays[f"in_{name}_dram"] = a
        args.append(nc.dram_tensor(f"in_{name}_dram", a.shape, _mybir.dt.from_np(a.dtype), kind="ExternalInput").ap())
    shape = arrays["in_L0_attn_x_dram"].shape
    args.append(nc.dram_tensor("out_0_dram", shape, _mybir.dt.float32, kind="ExternalOutput").ap())
    macaron_block(nc, *args)
    r = _run(nc, [arrays], core_ids=[0])
    return r.results[0]["out_0_dram"]
```

```python
from contextlib import ExitStack

import numpy as np

import concourse.bass as bass
from concourse import mybir

F32 = mybir.dt.float32
BF16 = mybir.dt.bfloat16
I32 = mybir.dt.int32
ALU = mybir.AluOpType
ACT = mybir.ActivationFunctionType
AX = mybir.AxisListType

P = 128
HEAD = 8
EPS = 1e-5
BIG = 3.0e38

TILES = 8
HALF = TILES // 2
SEQS = TILES // 2
CHUNK = TILES * P
BT = 4
BLOCK = BT * P
STEPS = 8
RING = 4
AHEAD = 5
FREE = 12

HBANK = [0, 1, 2, 0, 1, 2, 0, 1, 2, 0, 1, 2, 0, 1, 2, 1]


def back(pattern, at):
    n = len(pattern)
    return next(d for d in range(1, n + 1) if pattern[(at - d) % n] == pattern[at % n])


def macaron_block(nc, x, wq, wk, wv, wo, gate_w, gate_b, w1, b1, w2, b2, ws1, bs1, ws2, bs2, out):
    batch, seq, dim = x.shape
    experts, _, hidden = w1.shape
    HC = hidden // P
    NX = experts + 1
    SH = experts
    tokens = batch * seq
    groups = 2
    chunks = tokens // CHUNK
    per_group = chunks // groups
    gtok = tokens // groups
    SHARED = gtok // BLOCK
    ROUTED = (2 * gtok - experts) // BLOCK + experts
    NB = per_group * STEPS
    LATE = (0, 0, 0, 2)
    ROUTED_AT = [NB - ROUTED - late for late in LATE]
    RT = ROUTED
    assert dim == P and seq == 2 * P and HC == 4
    assert all(SHARED - late <= at < STEPS + AHEAD for late, at in zip(LATE, ROUTED_AT))
    CAP = gtok + BLOCK
    DUMMY = experts * CAP
    SROW = DUMMY + BLOCK
    NR = SROW + gtok
    NE = 4 * NB + 8
    K2 = 2 * TILES
    E_BASE = float(np.exp(1.0))
    EXP_BASE = float(np.exp(1.0 / np.sqrt(HEAD)))

    with ExitStack() as ctx:
        def sb(name, shape, dt=F32):
            return ctx.enter_context(nc.sbuf_tensor(name, shape, dt))

        def sem(name):
            return ctx.enter_context(nc.semaphore(name))

        def psum(name, shape, dt=F32):
            return ctx.enter_context(nc.psum_tensor(name, shape, dt))

        xbuf = nc.dram_tensor("slots_in", [4 * NR, 2 * P], BF16, kind="Internal").ap()
        ybuf = [nc.dram_tensor(f"slots_out{g}", [NB * BLOCK, P], F32, kind="Internal").ap() for g in range(groups)]

        X = sb("X", [P, chunks * TILES, P])
        w1h = sb("w1h", [P, NX, hidden], BF16)
        w1l = sb("w1l", [P, NX, hidden], BF16)
        w2h = sb("w2h", [P, NX, HC * P], BF16)
        w2l = sb("w2l", [P, NX, HC * P], BF16)
        b1row = sb("b1row", [NX * HC, P])
        b1t = sb("b1t", [P, NX * HC])
        b2row = sb("b2row", [NX, P])
        b2t = sb("b2t", [P, NX])
        wst = sb("wst", [P, 2, 2, hidden])
        watt = sb("watt", [P, 4, P])
        wqT = sb("wqT", [P, P])
        wkT = sb("wkT", [P, P])
        woT = sb("woT", [P, P])
        gw = sb("gw", [P, experts])
        gb = sb("gb", [P, experts])
        idf = sb("idf", [P, P])
        idb = sb("idb", [P, P], BF16)
        onesb = sb("onesb", [P, P], BF16)
        upper = sb("upper", [P, P], BF16)
        mask = sb("mask", [P, P])
        rev = sb("rev", [P, experts])
        ecap = sb("ecap", [P, experts])
        mhalf = sb("mhalf", [P, TILES])
        ebase = sb("ebase", [P, TILES])
        expbase = sb("expbase", [P, SEQS * HEAD])
        tri = sb("tri", [1, experts, experts])
        nidx = sb("nidx", [1, RT])
        zero = sb("zero", [P, BT, 2 * P], BF16)
        xin = sb("xin", [P, RING, BT, 2 * P], BF16)
        xT = sb("xT", [P, RING, 2, BLOCK], BF16)
        g32 = sb("g32", [P, 2, HC, BLOCK])
        gh = sb("gh", [P, 2, HC, BLOCK], BF16)
        gl = sb("gl", [P, 2, HC, BLOCK], BF16)
        yT = sb("yT", [P, 2, BLOCK])
        yout = sb("yout", [P, RING, BT, P])
        etab = sb("etab", [1, NE], I32)
        rtab = sb("rtab", [1, NE], I32)
        st6 = sb("st6", [P, TILES, 6])
        mv = sb("mv", [P, TILES, 2])
        ve = sb("ve", [P, TILES])
        rstd = sb("rstd", [P, TILES])
        xn = sb("xn", [P, TILES, P])
        xnT = sb("xnT", [P, CHUNK])
        xhl = sb("xhl", [P, 2, TILES, 2 * P], BF16)
        lg = sb("lg", [P, TILES, experts])
        lg2 = sb("lg2", [P, TILES, experts])
        cand = sb("cand", [P, TILES, experts])
        m12 = sb("m12", [P, 2, TILES])
        first = sb("first", [P, TILES])
        oh = sb("oh", [P, 2, TILES, experts])
        assign = sb("assign", [P, TILES, experts], BF16)
        asum = sb("asum", [P, experts], BF16)
        arow = sb("arow", [P, experts])
        dlog = sb("dlog", [P, TILES])
        edl = sb("edl", [P, TILES])
        den = sb("den", [P, TILES])
        rden = sb("rden", [P, TILES])
        rk = sb("rk", [P, TILES, experts])
        pick = sb("pick", [P, 2, TILES, experts])
        idx = sb("idx", [P, 2, K2], I32)
        pos = sb("pos", [P, per_group, K2])
        posge = sb("posge", [P, per_group * K2, experts])
        shift = sb("shift", [P, per_group * K2])
        hop = sb("hop", [P, experts])
        gix = sb("gix", [P, chunks, K2], I32)
        gidx = sb("gidx", [P, 2, K2], I32)
        wts = sb("wts", [P, 2, chunks * TILES])
        yg = sb("yg", [P, 2, K2, P])
        ysh = sb("ysh", [P, TILES, P])
        gram = sb("gram", [P, SEQS, P])
        gA = sb("gA", [P, SEQS, P])
        gm = sb("gm", [P, SEQS, P])
        hd = sb("hd", [P, SEQS, HEAD])
        hd2 = sb("hd2", [P, SEQS, HEAD])
        hmx = sb("hmx", [P, SEQS])
        hex_ = sb("hex", [P, SEQS, HEAD])
        hsum = sb("hsum", [P, SEQS])
        hrec = sb("hrec", [P, SEQS])
        hp = sb("hp", [P, SEQS, HEAD])
        prob = sb("prob", [P, SEQS, P])
        cT = sb("cT", [P, SEQS, P])
        weff = sb("weff", [P, SEQS, P])
        cnt = sb("cnt", [P, experts])
        padf = sb("padf", [1, experts])
        padrow = sb("padrow", [1, experts], I32)
        cnt_i = sb("cnt_i", [P, experts], I32)
        nb_i = sb("nb_i", [P, experts], I32)
        nb = sb("nb", [P, experts])
        cumm = sb("cumm", [1, experts, experts])
        cum = sb("cum", [1, experts])
        le = sb("le", [1, RT, experts])
        le2 = sb("le2", [1, RT, experts])
        en = sb("en", [1, RT])
        cp = sb("cp", [1, RT])
        bi = sb("bi", [1, RT])
        ok = sb("ok", [1, RT])
        bo = sb("bo", [1, RT])
        ro = sb("ro", [1, RT])

        hps = [psum(f"hps{i}", [P, BLOCK]) for i in range(3)]
        ytps = psum("ytps", [P, BLOCK])
        yps = psum("yps", [P, BT, P])
        tps = psum("tps", [P, 2, BT, P], BF16)
        c0 = psum("c0", [P, HALF, P])
        c1 = psum("c1", [P, SEQS, P])

        xload = [sem(f"xload{i}") for i in range(per_group + 1)]
        wload = [sem(f"wload{i}") for i in range(2)]
        w_hi, w_lo = sem("w_hi"), sem("w_lo")
        aload = sem("aload")
        const_ready, pool_order = sem("const_ready"), sem("pool_order")
        wT_ready, wT_sb = sem("wT_ready"), sem("wT_sb")
        zero_ready = sem("zero_ready")
        block_in = [sem(f"block_in{i}") for i in range(RING)]
        turned, xT_ready = sem("turned"), sem("xT_ready")
        up_done, gelu_done = sem("up_done"), sem("gelu_done")
        hi0_done, hi1_done, lo_done = sem("hi0_done"), sem("hi1_done"), sem("lo_done")
        down_done, yT_ready, y_turned, y_ready = sem("down_done"), sem("yT_ready"), sem("y_turned"), sem("y_ready")
        y_stored = [sem(f"y_stored{i}") for i in range(RING)]
        dve_order = sem("dve_order")
        var_ready, rstd_ready, xn_ready = sem("var_ready"), sem("rstd_ready"), sem("xn_ready")
        xn_turned, xnT_ready = sem("xn_turned"), sem("xnT_ready")
        split_hi, split_lo = sem("split_hi"), sem("split_lo")
        gate_done, assign_ready, rank_done = sem("gate_done"), sem("assign_ready"), sem("rank_done")
        dlog_ready, edl_ready, idx_ready = sem("dlog_ready"), sem("edl_ready"), sem("idx_ready")
        scattered, shared_stored = [[sem(f"{what}{i}") for i in range(2)] for what in ("scattered", "shared_stored")]
        sums_ready, count_done, table_ready, padded = sem("sums_ready"), sem("count_done"), sem("table_ready"), sem("padded")
        gidx_ready, gathered = sem("gidx_ready"), [sem(f"gathered{i}") for i in range(2)]
        shared_back, combined = sem("shared_back"), sem("combined")
        gram_done, gram_sb, a_done, a_sb = sem("gram_done"), sem("gram_sb"), sem("a_done"), sem("a_sb")
        scores_done, hd_ready, exp_ready, prob_ready = sem("scores_done"), sem("hd_ready"), sem("exp_ready"), sem("prob_ready")
        ct_done, ct_sb, weff_done, weff_sb = sem("ct_done"), sem("ct_sb"), sem("weff_done"), sem("weff_sb")
        att_done, att_added = sem("att_done"), sem("att_added")
        stored, passed = sem("stored"), sem("passed")

        x_v = x.rearrange("(c b) (p j) d -> c p b j d", b=SEQS, j=2)

        def norm_count(L, s, which):
            if L < 2:
                return s + L * per_group
            return s * 2 + (2 * per_group + (L - 2) * 2 * per_group + which)

        def plan(L, s):
            first = isinstance(s, int)
            if L == 1:
                return dict(stats1=0, norm1=2, turn1=4, gate=6, route=7, rank=9, split=10, slots=11, weights=13)
            if first:
                tail = dict(route=0, rank=1, slots=2, weights=5) if L > 2 else {}
                tail.update(count=3, table=4)
                if L == 4:
                    tail.update(weights=10)
                    return dict(tail, combine0=11, combine1=12, combine2=13)
                return dict(tail, combine0=5, combine1=6, combine2=6, stats0=7, norm0=8, gram=8, ga=9, scores=10, turn0a=9,
                            turn0b=10, soft1=10, soft2=12, ct=13, weff=13, out=14, stats1=14, norm1=15, turn1=15, split=15,
                            gate=15)
            if L == 4:
                return dict(combine0=11, combine1=12, combine2=13)
            return dict(route=0, rank=1, combine0=1, slots=2, combine1=2, combine2=3, stats0=3, weights=4, norm0=4, gram=5,
                        ga=6, scores=7, turn0a=7, turn0b=8, soft1=7, soft2=9, ct=10, weff=11, out=12, stats1=12, norm1=13,
                        turn1=14, split=14, gate=15)

        def place(L, s, parts):
            at = plan(L, s)
            halves = [[] for _ in range(2 * STEPS)]
            for name, part in parts:
                if name in at:
                    halves[at[name]].append(part)
            return halves

        def tail_of(L, s):
            if L == 1:
                return L, s
            return (L - 1, per_group - 1) if isinstance(s, int) else (L, s - 1)

        def iterations(eng, L, body):
            if L > 1:
                body(L, 0)
            with eng.Fori(1 if L > 1 else 0, per_group) as s:
                body(L, s)

        def chunk_of(L, s):
            return s + (L % groups) * per_group

        def parity(L, s):
            return (s + 1) % 2 if L == 0 else 0

        def wait_apart(eng, sem, value):
            eng.wait_ge(sem, value)
            eng.sem_inc(passed, 1)

        def batch(s):
            return range(2 * s, 2 * s + 2)

        def look_up(eng, table, n, most):
            return nc.values_load(table[0:1, bass.ds(n, 1)], engines=[eng.engine], min_val=0, max_val=most,
                                  skip_runtime_bounds_check_because="the table is built from counts that bound its values")

        def first_buffer(L):
            return (L * per_group) - 2

        def buffer_free(eng, sems, per_stage, L, s):
            if L == 0:
                if s >= 2:
                    eng.wait_ge(sems[parity(L, s)], per_stage + (0 if parity(L, s) else 16))
            else:
                eng.wait_ge(sems[0], s * per_stage + (first_buffer(L) * per_stage + 16))

        block = ctx.enter_context(nc.Block())

        @block.sync
        def _(sp):
            for t in range(RING):
                sp.sem_inc(y_stored[t], 16)
            sp.sem_inc(turned, FREE)
            sp.sem_inc(shared_stored[0], 16)

            def load_x(c):
                sp.dma_start(X[:, c * TILES:(c + 1) * TILES, :].rearrange("p (b j) d -> p b j d", b=SEQS),
                             x_v[c]).then_inc(xload[min(c, per_group)], 16)

            def load_expert(n):
                e = SH if n == 0 else n - 1
                if n >= 2:
                    sp.wait_ge(w_lo, 2 * (n - 1))
                sp.dma_start(wst[:, n % 2, 0, :], ws1 if e == SH else w1[e]).then_inc(wload[n % 2], 16)
                sp.dma_start(wst[:, n % 2, 1, :].rearrange("p (j d) -> p j d", j=HC),
                             (ws2 if e == SH else w2[e]).rearrange("(j p) d -> p j d", p=P)).then_inc(wload[n % 2], 16)

            def store_shared(L, s):
                wait_apart(sp, split_lo, s + (L * per_group + 1))
                row = s * CHUNK + ((L * NR) + SROW)
                sp.dma_start(xbuf[bass.ds(row, CHUNK), :].rearrange("(p t) d -> p t d", t=TILES),
                             xhl[:, parity(L, s), :, :]).then_inc(shared_stored[parity(L, s)], 16)

            def load_block(n, slot):
                if not isinstance(n, int) or n >= RING:
                    wait_apart(sp, turned, n + (FREE - RING + 1))
                row = look_up(sp, rtab, n, 4 * NR - BLOCK)
                sp.dma_start(xin[:, slot, :, :], xbuf[bass.ds(row, BLOCK), :].rearrange("(p j) d -> p j d", j=BT))\
                    .then_inc(block_in[slot], 16)

            def store_block(L, s, u):
                n = s * STEPS + ((L - 1) * NB + u)
                wait_apart(sp, y_ready, n + (1 + FREE))
                row = s * (STEPS * BLOCK) + u * BLOCK
                sp.dma_start(ybuf[(L - 1) % groups][bass.ds(row, BLOCK), :].rearrange("(p j) d -> p j d", j=BT),
                             yout[:, u % RING, :, :]).then_inc(y_stored[u % RING], 16)

            def pad_slots(L):
                sp.wait_ge(table_ready, L + 1)
                for e in range(experts):
                    row = look_up(sp, padrow, e, 4 * NR - BLOCK)
                    sp.dma_start(xbuf[bass.ds(row, BLOCK), :].rearrange("(p j) d -> p j d", j=BT), zero[:, :, :])\
                        .then_inc(padded, 16)
                sp.wait_ge(padded, 16 * experts * (L + 1))

            def fetch_shared(L, s):
                row = s * CHUNK
                if isinstance(s, int) and row >= (SHARED - LATE[L - 2]) * BLOCK:
                    row += (NB - SHARED) * BLOCK
                wait_apart(sp, combined, s + ((L - 2) * per_group + FREE))
                sp.dma_start(ysh[:, :, :], ybuf[L % groups][bass.ds(row, CHUNK), :].rearrange("(p t) d -> p t d", t=TILES))\
                    .then_inc(shared_back, 16)

            def store_chunk(L, s):
                c = chunk_of(L, s)
                wait_apart(sp, combined, s + ((L - 2) * per_group + FREE + 1))
                for b in range(SEQS):
                    src = X[:, bass.ds(c * TILES + 2 * b, 2), :]
                    dst = out[bass.ds(c * SEQS + b, 1)].rearrange("a (p j) d -> (a p) j d", j=2)
                    sp.dma_start(dst, src).then_inc(stored, 16)

            for c in range(per_group):
                load_x(c)
                if c == 0:
                    for n, w in enumerate((wq, wk, wv, wo)):
                        sp.dma_start(watt[:, n, :], w).then_inc(aload, 16)
                    sp.dma_start(gw[:, :], gate_w).then_inc(aload, 16)
                    sp.dma_start(gb[:, :], gate_b.rearrange("(a e) -> a e", a=1).to_broadcast([P, experts])).then_inc(aload, 16)
                    sp.dma_start(b1row[0:experts * HC, :], b1.rearrange("e (j p) -> (e j) p", p=P)).then_inc(aload, 16)
                    sp.dma_start(b1row[experts * HC:NX * HC, :], bs1.rearrange("(j p) -> j p", p=P)).then_inc(aload, 16)
                    sp.dma_start(b2row[0:experts, :], b2).then_inc(aload, 16)
                    sp.dma_start(b2row[experts:NX, :], bs2.rearrange("(a d) -> a d", a=1)).then_inc(aload, 16)
            load_expert(0)
            load_expert(1)
            for c in range(per_group, chunks):
                load_x(c)
            sp.wait_ge(const_ready, 1)
            for g in range(1, 4):
                sp.dma_start(xbuf[g * NR + DUMMY:g * NR + DUMMY + BLOCK, :].rearrange("(p j) d -> p j d", j=BT),
                             zero[:, :, :]).then_inc(zero_ready, 16)
            for s in range(per_group):
                store_shared(0, s)
                for n in batch(s):
                    if n + 2 < NX:
                        load_expert(n + 2)
                if s == 1:
                    for i in range(2):
                        sp.wait_ge(shared_stored[i], 16 + (0 if i else 16))
                    sp.wait_ge(const_ready, 2)
                    for n in range(RING):
                        load_block(n, n)
            sp.wait_ge(zero_ready, 48)
            for i in range(2):
                sp.wait_ge(shared_stored[i], 32 + (0 if i else 16))
            sp.wait_ge(scattered[0], 16)
            sp.wait_ge(scattered[1], 2 * 16 * K2)
            for n in range(RING, AHEAD):
                load_block(n, n % RING)

            def blocks_and_chunks(L, s):
                first = isinstance(s, int)
                if L < 4:
                    wait_apart(sp, shared_stored[0], s * 16 + (16 * (first_buffer(L) + 1)))
                if L >= 2 and not first:
                    fetch_shared(L, s)
                for u in range(STEPS):
                    n = s * STEPS + ((L - 1) * NB + u)
                    if L >= 2 and first and u == 1:
                        for t in range(RING):
                            sp.wait_ge(y_stored[t], 16 * (NB // RING * (L - 1) + 1 + (t < u)))
                        fetch_shared(L, s)
                    if u + AHEAD == ROUTED_AT[L - 1]:
                        if L == 1:
                            wait_apart(sp, scattered[0], s * (16 * K2) + (16 * K2 * first_buffer(L) + 16))
                        elif first:
                            pad_slots(L - 1)
                            sp.wait_ge(scattered[0], 16 * K2 * first_buffer(L) + 16)
                    load_block(n + AHEAD, (u + AHEAD) % RING)
                    store_block(L, s, u)
                if L < 4:
                    store_shared(L, s)
                else:
                    store_chunk(L, s)

            pad_slots(0)
            for L in range(1, 5):
                iterations(sp, L, blocks_and_chunks)
            for t in range(RING):
                sp.wait_ge(y_stored[t], 16 * (NB // RING * 4 + 1))
            for s in range(per_group):
                fetch_shared(5, s)
                store_chunk(5, s)
            sp.wait_ge(stored, 16 * SEQS * chunks)
            for t in range(RING):
                sp.wait_ge(y_stored[t], 16 * (NB // RING * 4 + 1))
            for t in range(RING):
                sp.wait_ge(block_in[t], 16 * (NB // RING * 4 + 1 + (t < AHEAD - RING)))

        @block.gpsimd
        def _(pool):
            pool.memset(zero[:, :, :], 0.0).then_inc(const_ready, 1)
            order = [0]

            def put(inst):
                order[0] += 1
                inst.then_inc(pool_order, 1)
            put(pool.memset(mhalf[:, :], -0.5))
            put(pool.memset(ebase[:, :], E_BASE))
            put(pool.memset(idf[:, :], 0.0))
            put(pool.memset(idb[:, :], 0.0))
            put(pool.memset(etab[:, :], SH))
            put(pool.memset(onesb[:, :], 1.0))
            put(pool.memset(upper[:, :], 0.0))
            put(pool.memset(mask[:, :], 1.0))
            put(pool.memset(tri[:, :, :], 1.0))
            put(pool.memset(expbase[:, :], EXP_BASE))
            put(pool.memset(asum[:, :], 0.0))
            put(pool.memset(rtab[:, :], DUMMY))
            put(pool.iota(rev[:, :], [[-1, experts]], base=experts, channel_multiplier=0, allow_small_or_imprecise_dtypes=True))
            put(pool.iota(ecap[:, :], [[CAP, experts]], base=0, channel_multiplier=0, allow_small_or_imprecise_dtypes=True))
            put(pool.iota(nidx[:, :], [[1, RT]], base=0, channel_multiplier=0, allow_small_or_imprecise_dtypes=True))
            pool.wait_ge(pool_order, order[0])
            for g in range(4):
                early = SHARED - LATE[g]
                put(pool.iota(rtab[:, g * NB:g * NB + early], [[BLOCK, early]], base=g * NR + SROW, channel_multiplier=0))
                if LATE[g]:
                    put(pool.iota(rtab[:, (g + 1) * NB - LATE[g]:(g + 1) * NB], [[BLOCK, LATE[g]]],
                                  base=g * NR + SROW + early * BLOCK, channel_multiplier=0))
            for m in (idf, idb):
                put(pool.affine_select(out=m[:, :], in_=m[:, :], compare_op=ALU.not_equal, fill=1.0, base=0,
                                       pattern=[[-1, P]], channel_multiplier=1))
            put(pool.affine_select(out=upper[:, :], in_=upper[:, :], compare_op=ALU.is_ge, fill=1.0, base=0,
                                   pattern=[[-1, P]], channel_multiplier=1))
            put(pool.affine_select(out=tri[:, :, :], in_=tri[:, :, :], compare_op=ALU.is_ge, fill=0.0, base=0,
                                   pattern=[[1, experts], [-1, experts]], channel_multiplier=0))
            mk = mask[:, :].rearrange("p (k i) -> p k i", i=HEAD)
            put(pool.affine_select(out=mk, in_=mk, compare_op=ALU.is_ge, fill=0.0, base=0,
                                   pattern=[[-HEAD, P // HEAD], [0, HEAD]], channel_multiplier=1))
            pool.wait_ge(pool_order, order[0])
            pool.affine_select(out=mk, in_=mk, compare_op=ALU.is_ge, fill=0.0, base=HEAD - 1,
                               pattern=[[HEAD, P // HEAD], [0, HEAD]], channel_multiplier=-1).then_inc(const_ready, 1)
            pool.dma_start(xbuf[DUMMY:DUMMY + BLOCK, :].rearrange("(p j) d -> p j d", j=BT), zero[:, :, :]).then_inc(scattered[0], 16)
            pool.sem_inc(combined, FREE)

            def root(n):
                pool.wait_ge(var_ready, n + 1)
                pool.tensor_tensor(rstd[:, :], ve[:, :], mhalf[:, :], ALU.pow).then_inc(rstd_ready, 1)

            def gate_exp(r):
                pool.wait_ge(dlog_ready, r + 1)
                pool.tensor_tensor(edl[:, :], ebase[:, :], dlog[:, :], ALU.pow).then_inc(edl_ready, 1)

            def head_exp(t):
                pool.wait_ge(hd_ready, t + 1)
                pool.tensor_tensor(hex_[:, :, :], expbase[:, :].rearrange("p (b i) -> p b i", b=SEQS), hd2[:, :, :], ALU.pow)\
                    .then_inc(exp_ready, 1)

            def scatter(r, par, rows=range(K2)):
                if rows[0] == 0:
                    pool.wait_ge(split_lo, r + 1)
                    wait_apart(pool, idx_ready, r + 1)
                for a in rows:
                    pool.indirect_dma_start(xbuf[:, :], bass.IndirectOffsetOnAxis(idx[:, par, a:a + 1], 0),
                                            xhl[:, par, a % TILES, :], None).then_inc(scattered[par], 16)

            def gather(L, s, par=0, rows=range(K2)):
                k = s + (L - 2) * per_group
                c = chunk_of(L, s)
                if rows[0] == 0:
                    pool.wait_ge(combined, k + (FREE - (1 if L == 5 and s > 0 else 0)))
                    pool.tensor_copy(gidx[:, par, :], gix[:, bass.ds(c, 1), :].rearrange("p a k -> p (a k)"))\
                        .then_inc(gidx_ready, 1)
                    wait_apart(pool, gidx_ready, k + 1)
                for a in rows:
                    pool.indirect_dma_start(yg[:, par, a, :], None, ybuf[L % groups][:, :],
                                            bass.IndirectOffsetOnAxis(gidx[:, par, a:a + 1], 0)).then_inc(gathered[par], 16)

            root(norm_count(0, 0, 1))
            for s in range(per_group):
                gate_exp(s)
                if s < per_group - 1:
                    root(norm_count(0, s + 1, 1))
                    scatter(s, parity(0, s))
            with pool.Fori(0, per_group) as s:
                root(norm_count(1, s, 1))
                scatter(s + (per_group - 1), 0)
                gate_exp(s + per_group)
            def part(a, b):
                return range(a * K2 // 8, b * K2 // 8)

            def outputs_stored(L):
                pool.wait_ge(table_ready, L - 1)
                for t in range(RING):
                    late = 1 if t >= RING - LATE[L - 2] else 0
                    pool.wait_ge(y_stored[t], 16 * (NB // RING * (L - 1) + 1 - late))

            for L in range(2, 4):
                outputs_stored(L)
                gather(L, 0)
                if L > 2:
                    gate_exp(L * per_group - 1)
                scatter(L * per_group - 1, 0, part(0, 3))
                root(norm_count(L, 0, 0))
                scatter(L * per_group - 1, 0, part(3, 8))
                head_exp((L - 2) * per_group)
                gather(L, 1, 0, part(0, 1))
                root(norm_count(L, 0, 1))
                gather(L, 1, 0, part(1, 8))

                def rest(s, last):
                    r = s + (L * per_group - 1)
                    gate_exp(r)
                    scatter(r, 0, part(0, 2))
                    root(norm_count(L, s, 0))
                    scatter(r, 0, part(2, 5))
                    head_exp(s + (L - 2) * per_group)
                    scatter(r, 0, part(5, 8))
                    if not last:
                        gather(L, s + 1, 0, part(0, 1))
                    root(norm_count(L, s, 1))
                    if not last:
                        gather(L, s + 1, 0, part(1, 8))
                with pool.Fori(1, per_group - 1) as s:
                    rest(s, False)
                rest(per_group - 1, True)
            scatter(4 * per_group - 1, 0)
            gate_exp(4 * per_group - 1)
            outputs_stored(4)
            with pool.Fori(0, per_group) as s:
                gather(4, s)
            outputs_stored(5)
            for s in range(per_group):
                gather(5, s, s % 2)
            pool.wait_ge(scattered[0], 16 + 16 * K2 * first_buffer(4))

        @block.tensor
        def _(pe):
            pe.wait_ge(aload, 160)
            pe.wait_ge(const_ready, 2)
            for n, m in enumerate((0, 1, 3)):
                pe.transpose(c0[:, n, :], watt[:, m, :], idf[:, :])
            pe.transpose(c0[:, 3, 0:NX * HC], b1row[:, :], idf[0:NX * HC, 0:NX * HC])
            pe.transpose(c0[:, 3, NX * HC:NX * HC + NX], b2row[:, :], idf[0:NX, 0:NX]).then_inc(wT_ready, 1)
            pe.wait_ge(wT_sb, 5)

            def turn_half(n, h, bank=None):
                pe.wait_ge(xn_ready, n + 1)
                if h == 1 and bank is None:
                    pe.wait_ge(xnT_ready, n * 2 + 1)
                for t in range(HALF):
                    last = pe.transpose((bank or c0)[:, t, :], xn[:, h * HALF + t, :], idf[:, :])
                last.then_inc(xn_turned, 1)

            def turn_both(n):
                turn_half(n, 0)
                turn_half(n, 1, c1)

            def gate(n, r):
                pe.wait_ge(xnT_ready, n * 2 + 2)
                for t in range(TILES):
                    last = pe.matmul(c1[:, 0, t * experts:(t + 1) * experts], xnT[:, t * P:(t + 1) * P], gw[:, :],
                                     start=True, stop=True)
                last.then_inc(gate_done, 1)

            def rank(r):
                pe.wait_ge(assign_ready, r + 1)
                o = c1[:, 0, 0:TILES * experts].rearrange("p (t e) -> p t e", t=TILES)
                pe.matmul(o, upper[:, :], assign[:, :, :], start=True, stop=False)
                pe.matmul(o, onesb[:, :], asum[:, :].unsqueeze(1).to_broadcast([P, TILES, experts]), start=False, stop=False)
                for t in range(1, TILES):
                    last = pe.matmul(o[:, t:, :], onesb[:, :], assign[:, 0:TILES - t, :], start=False, stop=t == TILES - 1)
                last.then_inc(rank_done, 1)

            def count(L):
                pe.wait_ge(sums_ready, L + 1)
                pe.matmul(c1[:, 0, 0:experts], onesb[:, :], asum[:, :], start=True, stop=True).then_inc(count_done, 1)

            def att_gram(n, t):
                pe.wait_ge(xn_ready, n + 1)
                for b in range(SEQS):
                    for j in range(2):
                        v = xn[:, 2 * b + j, :]
                        last = pe.matmul(c1[:, b, :], v, v, start=j == 0, stop=j == 1)
                last.then_inc(gram_done, 1)

            def att_product(ready, t, lhsT, rhs, done):
                pe.wait_ge(ready, t + 1)
                for b in range(SEQS):
                    last = pe.matmul(c1[:, b, :], lhsT[:, b, :], rhs, start=True, stop=True)
                last.then_inc(done, 1)

            def att_out(n, t):
                pe.wait_ge(weff_sb, t + 1)
                pe.wait_ge(xnT_ready, n * 2 + 2)
                for h, bank in enumerate((c0, c1)):
                    for a in range(HALF):
                        tile = h * HALF + a
                        last = pe.matmul(bank[:, a, :], xnT[:, tile * P:(tile + 1) * P], weff[:, tile // 2, :],
                                         start=True, stop=True)
                    last.then_inc(att_done, 1)

            def turn_block(n, slot, landed):
                pe.wait_ge(block_in[slot], landed)
                pe.wait_ge(xT_ready, n + FREE)
                for h in range(2):
                    for j in range(BT):
                        last = pe.transpose(tps[:, h, j, :], xin[:, slot, j, h * P:(h + 1) * P], idb[:, :])
                last.then_inc(turned, 1)

            def up(n, u, e):
                slot = u % RING
                pe.wait_ge(xT_ready, n + FREE + 1)
                for j in range(HC):
                    at = HC * slot + j
                    bank = hps[HBANK[at]]
                    pe.wait_ge(gelu_done, n * HC + (j + 1 - back(HBANK, at) + FREE))
                    wh = w1h[:, bass.ds(e, 1), j * P:(j + 1) * P].rearrange("p a d -> p (a d)")
                    wl = w1l[:, bass.ds(e, 1), j * P:(j + 1) * P].rearrange("p a d -> p (a d)")
                    pe.matmul(bank[:, :], wh, xT[:, slot, 0, :], start=True, stop=False)
                    pe.matmul(bank[:, :], wh, xT[:, slot, 1, :], start=False, stop=False)
                    pe.matmul(bank[:, :], wl, xT[:, slot, 0, :], start=False, stop=True).then_inc(up_done, 1)

            def turn_y(n, u):
                pe.wait_ge(yT_ready, n + (1 + FREE))
                pe.wait_ge(y_ready, n + FREE)
                for t in range(BT):
                    last = pe.transpose(yps[:, t, :], yT[:, u % 2, t * P:(t + 1) * P], idf[:, :])
                last.then_inc(y_turned, 1)

            def down(n, u, e):
                g = u % 2
                pe.wait_ge(yT_ready, n + FREE)
                for j in range(HC):
                    if j == 0:
                        pe.wait_ge(hi0_done, n + 1)
                        pe.wait_ge(lo_done, n * 2 + 1)
                    if j == HC // 2:
                        pe.wait_ge(lo_done, n * 2 + 2)
                    wh = w2h[:, bass.ds(e, 1), j * P:(j + 1) * P].rearrange("p a d -> p (a d)")
                    wl = w2l[:, bass.ds(e, 1), j * P:(j + 1) * P].rearrange("p a d -> p (a d)")
                    pe.matmul(ytps[:, :], wh, gh[:, g, j, :], start=j == 0, stop=False)
                    pe.matmul(ytps[:, :], wh, gl[:, g, j, :], start=False, stop=False)
                    last = pe.matmul(ytps[:, :], wl, gh[:, g, j, :], start=False, stop=j == HC - 1)
                last.then_inc(down_done, 1)

            pe.sem_inc(down_done, FREE)
            for s in range(per_group):
                n1 = norm_count(0, s, 1)
                turn_both(n1)
                if s == per_group - 1:
                    turn_block(2, 2, 16)
                    up(1, 1, SH)
                gate(n1, s)
                if s == per_group - 1:
                    down(0, 0, SH)
                rank(s)
                if s == per_group - 2:
                    pe.wait_ge(w_lo, 2)
                    turn_block(0, 0, 16)
                    turn_block(1, 1, 16)
                    up(0, 0, SH)
            count(0)
            pe.wait_ge(w_lo, 2 * NX)

            def blocks_and_chunks(L, s):
                first = isinstance(s, int)
                n0 = norm_count(L, s, 0)
                n1 = norm_count(L, s, 1)
                t_ = s + (L - 2) * per_group
                Lt, st = tail_of(L, s)
                pieces = place(L, s, [
                    ("rank", lambda: rank(st + Lt * per_group)),
                    ("count", lambda: count(L - 1)),
                    ("gram", lambda: att_gram(n0, t_)),
                    ("turn0a", lambda: turn_half(n0, 0)),
                    ("ga", lambda: att_product(gram_sb, t_, gram, wkT[:, :], a_done)),
                    ("turn0b", lambda: turn_half(n0, 1)),
                    ("scores", lambda: att_product(a_sb, t_, gA, wqT[:, :], scores_done)),
                    ("ct", lambda: att_product(prob_ready, t_, prob, watt[:, 2, :], ct_done)),
                    ("weff", lambda: att_product(ct_sb, t_, cT, woT[:, :], weff_done)),
                    ("out", lambda: att_out(n0, t_)),
                    ("turn1", lambda: turn_both(n1)),
                    ("gate", lambda: gate(n1, s + L * per_group))])
                e_next = look_up(pe, etab, s * STEPS + ((L - 1) * NB + 1), SH)
                for u in range(STEPS):
                    n = s * STEPS + ((L - 1) * NB + u)
                    if u == ROUTED_AT[L - 1] - 2 and (first or L == 1):
                        pe.wait_ge(table_ready, L)
                    e_down, e_next = e_next, look_up(pe, etab, n + 2, SH)
                    turn_block(n + 3, (u + 3) % RING, s * (16 * STEPS // RING) + 16 * ((L - 1) * NB // RING + (u + 3) // RING + 1))
                    up(n + 2, u + 2, e_next)
                    for piece in pieces[2 * u]:
                        piece()
                    turn_y(n, u)
                    down(n + 1, u + 1, e_down)
                    for piece in pieces[2 * u + 1]:
                        piece()

            for L in range(1, 5):
                iterations(pe, L, blocks_and_chunks)

        @block.scalar
        def _(act):
            act.wait_ge(wT_ready, 1)
            for n, m in enumerate((wqT, wkT, woT)):
                act.activation(m[:, :], c0[:, n, :], ACT.Copy).then_inc(wT_sb, 1)
            act.activation(b1t[:, :], c0[:, 3, 0:NX * HC], ACT.Copy).then_inc(wT_sb, 1)
            act.activation(b2t[:, :], c0[:, 3, NX * HC:NX * HC + NX], ACT.Copy).then_inc(wT_sb, 1)

            def weights_high(n):
                e = SH if n == 0 else n - 1
                act.wait_ge(wload[n % 2], 32 * (n // 2 + 1))
                act.activation(w1h[:, e, :], wst[:, n % 2, 0, :], ACT.Copy).then_inc(w_hi, 1)
                act.activation(w2h[:, e, :], wst[:, n % 2, 1, :], ACT.Copy).then_inc(w_hi, 1)

            def split_high(L, s):
                act.wait_ge(xn_ready, norm_count(L, s, 1) + 1)
                buffer_free(act, scattered, 16 * K2, L, s)
                buffer_free(act, shared_stored, 16, L, s)
                act.activation(xhl[:, parity(L, s), :, 0:P], xn[:, :, :], ACT.Copy).then_inc(split_hi, 1)

            def take_xnT(n, h, bank=None):
                act.wait_ge(xn_turned, n * 2 + (h + 2))
                act.activation(xnT[:, h * HALF * P:(h + 1) * HALF * P], (bank or c0)[:, :, :].rearrange("p t d -> p (t d)"), ACT.Copy)\
                    .then_inc(xnT_ready, 1)

            def take(done, t, dst, kept):
                act.wait_ge(done, t + 1)
                act.activation(dst[:, :, :], c1[:, :, :], ACT.Copy).then_inc(kept, 1)

            def gelus(n, u, js, e):
                slot = u % RING
                for j in js:
                    act.wait_ge(up_done, n * HC + (j + 1))
                    if j == 0:
                        act.wait_ge(down_done, n + (FREE - 1))
                    act.activation(g32[:, u % 2, j, :], hps[HBANK[HC * slot + j]][:, :], ACT.Gelu,
                                   bias=b1t[:, bass.ds(e * HC + j, 1)]).then_inc(gelu_done, 1)

            def high(n, u, half):
                act.wait_ge(gelu_done, n * HC + (2 * half + 2 + FREE))
                act.activation(gh[:, u % 2, 2 * half:2 * half + 2, :], g32[:, u % 2, 2 * half:2 * half + 2, :], ACT.Copy)\
                    .then_inc((hi0_done, hi1_done)[half], 1)

            def take_yT(n, u, e):
                act.wait_ge(down_done, n + (1 + FREE))
                act.wait_ge(y_turned, n + (FREE - 1))
                act.activation(yT[:, u % 2, :], ytps[:, :], ACT.Identity, bias=b2t[:, bass.ds(e, 1)]).then_inc(yT_ready, 1)

            def take_y(n, u, stored_before):
                act.wait_ge(y_turned, n + (1 + FREE))
                act.wait_ge(y_stored[u % RING], stored_before)
                act.activation(yout[:, u % RING, :, :], yps[:, :, :], ACT.Copy).then_inc(y_ready, 1)

            def hidden_values(n):
                gelus(n, n, (0, 1), SH)
                high(n, n, 0)
                gelus(n, n, (2, 3), SH)
                high(n, n, 1)

            act.sem_inc(xn_turned, 1)
            act.sem_inc(gelu_done, FREE)
            act.sem_inc(y_ready, FREE)
            act.sem_inc(yT_ready, FREE)
            act.sem_inc(y_turned, FREE)
            for s in range(per_group):
                split_high(0, s)
                take_xnT(norm_count(0, s, 1), 0)
                take_xnT(norm_count(0, s, 1), 1, c1)
                for n in batch(s):
                    weights_high(n)
                if s == per_group - 1:
                    hidden_values(1)
                if s == per_group - 2:
                    hidden_values(0)
            for n in range(2 * per_group, NX):
                weights_high(n)
            take_yT(0, 0, SH)

            def blocks_and_chunks(L, s):
                first = isinstance(s, int)
                n0 = norm_count(L, s, 0)
                n1 = norm_count(L, s, 1)
                t_ = s + (L - 2) * per_group
                pieces = place(L, s, [
                    ("gram", lambda: take(gram_done, t_, gram, gram_sb)),
                    ("turn0a", lambda: take_xnT(n0, 0)),
                    ("ga", lambda: take(a_done, t_, gA, a_sb)),
                    ("turn0b", lambda: take_xnT(n0, 1)),
                    ("ct", lambda: take(ct_done, t_, cT, ct_sb)),
                    ("weff", lambda: take(weff_done, t_, weff, weff_sb)),
                    ("turn1", lambda: (take_xnT(n1, 0), take_xnT(n1, 1, c1))),
                    ("split", lambda: split_high(L, s))])
                e_next = look_up(act, etab, s * STEPS + ((L - 1) * NB + 1), SH)
                for u in range(STEPS):
                    n = s * STEPS + ((L - 1) * NB + u)
                    if u == ROUTED_AT[L - 1] - 2 and (first or L == 1):
                        act.wait_ge(table_ready, L)
                    e_down, e_next = e_next, look_up(act, etab, n + 2, SH)
                    gelus(n + 2, u + 2, (0, 1), e_next)
                    high(n + 2, u + 2, 0)
                    gelus(n + 2, u + 2, (2, 3), e_next)
                    high(n + 2, u + 2, 1)
                    for piece in pieces[2 * u]:
                        piece()
                    take_y(n, u, s * (16 * STEPS // RING) + 16 * ((L - 1) * NB // RING + u // RING + 1))
                    take_yT(n + 1, u + 1, e_down)
                    for piece in pieces[2 * u + 1]:
                        piece()

            for L in range(1, 5):
                iterations(act, L, blocks_and_chunks)

        @block.vector
        def _(dve):
            class Order:
                base, n = 0, 0

            def step(inst):
                Order.n += 1
                inst.then_inc(dve_order, 1)

            def settle():
                dve.wait_ge(dve_order, Order.base + Order.n)

            def weights_low(n):
                e = SH if n == 0 else n - 1
                dve.wait_ge(w_hi, 2 * n + 2)
                dve.tensor_tensor(w1l[:, e, :], wst[:, n % 2, 0, :], w1h[:, e, :], ALU.subtract).then_inc(w_lo, 1)
                dve.tensor_tensor(w2l[:, e, :], wst[:, n % 2, 1, :], w2h[:, e, :], ALU.subtract).then_inc(w_lo, 1)

            def tile_of(c, t):
                return X[:, bass.ds(c * TILES + t, 1), :].rearrange("p a d -> p (a d)")

            def stats(c, n):
                for t in range(TILES):
                    step(dve.bn_stats(st6[:, t, :], tile_of(c, t)))
                wait_apart(dve, dve_order, Order.base + Order.n)
                for t in range(TILES):
                    step(dve.bn_aggr(mv[:, t, :], st6[:, t, :]))
                settle()
                dve.tensor_scalar(ve[:, :], mv[:, :, 1], EPS, None, ALU.add).then_inc(var_ready, 1)

            def normalise(c, n):
                dve.wait_ge(rstd_ready, n + 1)
                dve.wait_ge(xn_turned, n * 2 + 1)
                for t in range(TILES):
                    last = dve.tensor_scalar(xn[:, t, :], tile_of(c, t),
                                             mv[:, t, 0:1], rstd[:, t:t + 1], ALU.subtract, ALU.mult)
                last.then_inc(xn_ready, 1)

            def split_low(L, s):
                par = parity(L, s)
                dve.wait_ge(split_hi, s + (L * per_group + 1))
                dve.tensor_tensor(xhl[:, par, :, P:2 * P], xn[:, :, :], xhl[:, par, :, 0:P], ALU.subtract).then_inc(split_lo, 1)

            def over_e(ap):
                return ap.unsqueeze(2).to_broadcast([P, TILES, experts])

            def over_t(ap):
                return ap.unsqueeze(1).to_broadcast([P, TILES, experts])

            def choose(k, src):
                step(dve.reduce_max(m12[:, k, :], src, AX.X))
                settle()
                step(dve.tensor_tensor(cand[:, :, :], src, over_e(m12[:, k, :]), ALU.is_ge))
                settle()
                step(dve.tensor_tensor(cand[:, :, :], cand[:, :, :], over_t(rev[:, :]), ALU.mult))
                settle()
                step(dve.reduce_max(first[:, :], cand[:, :, :], AX.X))
                settle()
                step(dve.tensor_tensor(oh[:, k, :, :], over_t(rev[:, :]), over_e(first[:, :]), ALU.is_equal))
                settle()

            def route(L, s):
                dve.wait_ge(gate_done, s + (L * per_group + 1))
                step(dve.tensor_tensor(lg[:, :, :], c1[:, 0, 0:TILES * experts].rearrange("p (t e) -> p t e", t=TILES),
                                       over_t(gb[:, :]), ALU.add))
                settle()
                choose(0, lg[:, :, :])
                step(dve.scalar_tensor_tensor(lg2[:, :, :], oh[:, 0, :, :], -BIG, lg[:, :, :], ALU.mult, ALU.add))
                settle()
                choose(1, lg2[:, :, :])
                dve.tensor_tensor(assign[:, :, :], oh[:, 0, :, :], oh[:, 1, :, :], ALU.add).then_inc(assign_ready, 1)
                dve.tensor_tensor(dlog[:, :], m12[:, 1, :], m12[:, 0, :], ALU.subtract).then_inc(dlog_ready, 1)

            def slots(L, s):
                r = s + L * per_group
                dve.wait_ge(rank_done, r + 1)
                buffer_free(dve, scattered, 16 * K2, L, s)
                step(dve.tensor_tensor(rk[:, :, :], c1[:, 0, 0:TILES * experts].rearrange("p (t e) -> p t e", t=TILES),
                                       over_t(ecap[:, :]), ALU.add))
                dve.wait_ge(assign_ready, r + 1)
                step(dve.reduce_sum(arow[:, :], assign[:, :, :].rearrange("p t e -> p e t"), AX.X))
                settle()
                step(dve.tensor_tensor(pick[:, :, :, :], oh[:, :, :, :],
                                       rk[:, :, :].unsqueeze(1).to_broadcast([P, 2, TILES, experts]), ALU.mult))
                step(dve.tensor_tensor(asum[:, :], asum[:, :], arow[:, :], ALU.add))
                settle()
                here = pos[:, bass.ds(s, 1), :]
                step(dve.reduce_sum(here.rearrange("p a (k t) -> p (a k) t", k=2), pick[:, :, :, :], AX.X))
                settle()
                dve.tensor_scalar(idx[:, parity(L, s), :], here.rearrange("p a k -> p (a k)"), float(L * NR), None, ALU.add)\
                    .then_inc(idx_ready, 1)

            def weights(L, s):
                c = chunk_of(L, s)
                dve.wait_ge(edl_ready, s + (L * per_group + 1))
                step(dve.tensor_scalar(den[:, :], edl[:, :], 1.0, None, ALU.add))
                settle()
                step(dve.reciprocal(rden[:, :], den[:, :]))
                settle()
                w = [wts[:, k, bass.ds(c * TILES, TILES)] for k in range(2)]
                step(dve.tensor_scalar(w[0], rden[:, :], 0.5, None, ALU.mult))
                step(dve.scalar_tensor_tensor(w[1], edl[:, :], 0.5, rden[:, :], ALU.mult, ALU.mult))

            TAIL_STEPS = 12 + 5 + 4
            ROUTE_STEPS = 2 * TILES + TAIL_STEPS
            COMBINE_STEPS = 2 * TILES
            ATT_STEPS = 2 * TILES + 6 + 2

            def table(L):
                def bc(ap, n):
                    return ap.unsqueeze(1).to_broadcast([ap.shape[0], n, experts])
                routed = slice(L * NB + ROUTED_AT[L], L * NB + ROUTED_AT[L] + RT)
                dve.wait_ge(count_done, L + 1)
                step(dve.tensor_copy(cnt[:, :], c1[:, 0, 0:experts]))
                step(dve.memset(asum[:, :], 0.0))
                settle()
                step(dve.tensor_scalar(cnt_i[:, :], cnt[:, :], float(BLOCK - 1), None, ALU.add))
                step(dve.tensor_tensor(padf[:, :], cnt[0:1, :], ecap[0:1, :], ALU.add))
                settle()
                step(dve.tensor_scalar(padrow[:, :], padf[:, :], float(L * NR), None, ALU.add))
                step(dve.tensor_scalar(nb_i[:, :], cnt_i[:, :], BLOCK.bit_length() - 1, None, ALU.arith_shift_right))
                settle()
                step(dve.tensor_copy(nb[:, :], nb_i[:, :]))
                settle()
                step(dve.tensor_tensor(cumm[:, :, :], tri[:, :, :], bc(nb[0:1, :], experts), ALU.mult))
                settle()
                step(dve.reduce_sum(cum[:, :], cumm[:, :, :], AX.X))
                settle()
                step(dve.tensor_tensor(le[:, :, :], bc(cum[:, :], RT), nidx[:, :].unsqueeze(2).to_broadcast([1, RT, experts]),
                                       ALU.is_le))
                settle()
                step(dve.reduce_sum(en[:, :], le[:, :, :], AX.X))
                step(dve.tensor_tensor(le2[:, :, :], le[:, :, :], bc(nb[0:1, :], RT), ALU.mult))
                settle()
                step(dve.reduce_sum(cp[:, :], le2[:, :, :], AX.X))
                step(dve.tensor_scalar(ok[:, :], en[:, :], float(experts), float(BLOCK), ALU.is_lt, ALU.mult))
                settle()
                step(dve.tensor_tensor(bi[:, :], nidx[:, :], cp[:, :], ALU.subtract))
                settle()
                step(dve.tensor_tensor(bo[:, :], bi[:, :], ok[:, :], ALU.mult))
                step(dve.tensor_scalar(ro[:, :], en[:, :], float(CAP), float(L * NR), ALU.mult, ALU.add))
                step(dve.tensor_copy(etab[:, routed], en[:, :]))
                settle()
                step(dve.tensor_tensor(rtab[:, routed], ro[:, :], bo[:, :], ALU.add))
                step(dve.memset(hop[:, 0:1], float(ROUTED_AT[L] * BLOCK)))
                step(dve.tensor_scalar(hop[:, 1:experts], nb[:, 0:experts - 1], float(BLOCK), -float(CAP), ALU.mult, ALU.add))
                allpos = pos[:, :, :].rearrange("p c k -> p (c k)")
                n = per_group * K2
                step(dve.tensor_tensor(posge[:, :, :], allpos.unsqueeze(2).to_broadcast([P, n, experts]), bc(ecap[:, :], n), ALU.is_ge))
                settle()
                step(dve.tensor_tensor(posge[:, :, :], posge[:, :, :], bc(hop[:, :], n), ALU.mult))
                settle()
                step(dve.reduce_sum(shift[:, :], posge[:, :, :], AX.X))
                settle()
                g = L % groups
                dve.tensor_tensor(gix[:, g * per_group:(g + 1) * per_group, :].rearrange("p c k -> p (c k)"), allpos, shift[:, :],
                                  ALU.add).then_inc(table_ready, 1)

            TABLE_STEPS = 24

            def note_sums():
                settle()
                dve.tensor_copy(arow[:, 0:1], asum[:, 0:1]).then_inc(sums_ready, 1)

            def combine_choice(L, s, ch, par=0, times=None):
                k = s + (L - 2) * per_group
                c = chunk_of(L, s)
                if ch == 0:
                    dve.wait_ge(gathered[par], (k + 1 if times is None else times) * (16 * K2))
                else:
                    settle()
                for t in range(TILES):
                    xc = tile_of(c, t)
                    step(dve.scalar_tensor_tensor(xc, yg[:, par, ch * TILES + t, :], wts[:, ch, bass.ds(c * TILES + t, 1)],
                                                  xc, ALU.mult, ALU.add))

            def combine_shared(L, s):
                k = s + (L - 2) * per_group
                dve.wait_ge(shared_back, k * 16 + 16)
                settle()
                xa = X[:, bass.ds(chunk_of(L, s) * TILES, TILES), :]
                dve.scalar_tensor_tensor(xa, ysh[:, :, :], 0.5, xa, ALU.mult, ALU.add).then_inc(combined, 1)
                wait_apart(dve, combined, k + (1 + FREE))

            def att_soft1(t):
                dve.wait_ge(scores_done, t + 1)
                step(dve.tensor_tensor(gm[:, :, :], c1[:, :, :], mask[:, :].unsqueeze(1).to_broadcast([P, SEQS, P]), ALU.mult))
                settle()
                step(dve.reduce_sum(hd[:, :, :], gm[:, :, :].rearrange("p b (k i) -> p b i k", i=HEAD), AX.X))
                settle()
                step(dve.reduce_max(hmx[:, :], hd[:, :, :], AX.X))
                settle()
                dve.tensor_tensor(hd2[:, :, :], hd[:, :, :], hmx[:, :].unsqueeze(2).to_broadcast([P, SEQS, HEAD]), ALU.subtract)\
                    .then_inc(hd_ready, 1)

            def att_soft2(t):
                dve.wait_ge(exp_ready, t + 1)
                step(dve.reduce_sum(hsum[:, :], hex_[:, :, :], AX.X))
                settle()
                step(dve.reciprocal(hrec[:, :], hsum[:, :]))
                settle()
                step(dve.tensor_tensor(hp[:, :, :], hex_[:, :, :], hrec[:, :].unsqueeze(2).to_broadcast([P, SEQS, HEAD]), ALU.mult))
                settle()
                for b in range(SEQS):
                    last = dve.tensor_tensor(prob[:, b, :].rearrange("p (k i) -> p k i", i=HEAD),
                                             mask[:, :].rearrange("p (k i) -> p k i", i=HEAD),
                                             hp[:, b, :].unsqueeze(1).to_broadcast([P, P // HEAD, HEAD]), ALU.mult)
                last.then_inc(prob_ready, 1)

            def att_add(L, s, t):
                c = chunk_of(L, s)
                for h, bank in enumerate((c0, c1)):
                    dve.wait_ge(att_done, t * 2 + (h + 1))
                    xa = X[:, bass.ds(c * TILES + h * HALF, HALF), :]
                    dve.tensor_tensor(xa, bank[:, :, :], xa, ALU.add).then_inc(att_added, 1)
                wait_apart(dve, att_added, t * 2 + 2)

            ATT_STEPS -= 2

            def take_xT(n, u):
                dve.wait_ge(turned, n + (1 + FREE))
                dve.tensor_copy(xT[:, u % RING, :, :].rearrange("p h s -> p (h s)"),
                                tps[:, :, :, :].rearrange("p h a b -> p (h a b)")).then_inc(xT_ready, 1)

            def split_block(n, u):
                g = u % 2
                dve.wait_ge(hi0_done, n + 1)
                dve.tensor_tensor(gl[:, g, 0:2, :], g32[:, g, 0:2, :], gh[:, g, 0:2, :], ALU.subtract).then_inc(lo_done, 1)
                dve.wait_ge(hi1_done, n + 1)
                dve.tensor_tensor(gl[:, g, 2:4, :], g32[:, g, 2:4, :], gh[:, g, 2:4, :], ALU.subtract).then_inc(lo_done, 1)

            dve.sem_inc(xT_ready, FREE)
            dve.wait_ge(const_ready, 2)
            dve.wait_ge(xload[0], 16)
            stats(0, norm_count(0, 0, 1))
            for s in range(per_group):
                last = s == per_group - 1
                n1 = norm_count(0, s, 1)
                normalise(s, n1)
                split_low(0, s)
                if last:
                    split_block(0, 0)
                    take_xT(2, 2)
                if s > 0:
                    for n in batch(s):
                        weights_low(n)
                if s == 0:
                    dve.wait_ge(aload, 160)
                route(0, s)
                slots(0, s)
                if not last:
                    dve.wait_ge(xload[s + 1], 16)
                    stats(s + 1, n1 + 1)
                weights(0, s)
                if s == 0:
                    for n in batch(s):
                        weights_low(n)
                if s == per_group - 2:
                    take_xT(0, 0)
                    take_xT(1, 1)
            note_sums()
            for n in range(2 * per_group, NX):
                weights_low(n)
            split_block(1, 1)
            table(0)
            total = per_group * ROUTE_STEPS + TABLE_STEPS
            assert Order.n == total, (Order.n, total)
            dve.wait_ge(xload[per_group], 16 * per_group)

            def blocks_and_chunks(L, s):
                n0 = norm_count(L, s, 0)
                n1 = norm_count(L, s, 1)
                t_ = s + (L - 2) * per_group
                c = chunk_of(L, s)
                tail = tail_of(L, s)
                pieces = place(L, s, [
                    ("route", lambda: route(*tail)),
                    ("slots", lambda: slots(*tail)),
                    ("weights", lambda: weights(*tail)),
                    ("combine0", lambda: combine_choice(L, s, 0)),
                    ("combine1", lambda: combine_choice(L, s, 1)),
                    ("combine2", lambda: combine_shared(L, s)),
                    ("stats0", lambda: stats(c, n0)),
                    ("count", note_sums),
                    ("table", lambda: table(L - 1)),
                    ("norm0", lambda: normalise(c, n0)),
                    ("soft1", lambda: att_soft1(t_)),
                    ("soft2", lambda: att_soft2(t_)),
                    ("out", lambda: att_add(L, s, t_)),
                    ("stats1", lambda: stats(c, n1)),
                    ("norm1", lambda: normalise(c, n1)),
                    ("split", lambda: split_low(L, s))])
                for u in range(STEPS):
                    n = s * STEPS + ((L - 1) * NB + u)
                    take_xT(n + 3, u + 3)
                    for piece in pieces[2 * u]:
                        piece()
                    split_block(n + 2, u + 2)
                    for piece in pieces[2 * u + 1]:
                        piece()

            CHUNK_STEPS = {1: ROUTE_STEPS, 2: ROUTE_STEPS + COMBINE_STEPS + ATT_STEPS,
                           3: ROUTE_STEPS + COMBINE_STEPS + ATT_STEPS, 4: COMBINE_STEPS}
            FIRST_STEPS = {2: ROUTE_STEPS - TAIL_STEPS + COMBINE_STEPS + ATT_STEPS + TABLE_STEPS,
                           3: ROUTE_STEPS + COMBINE_STEPS + ATT_STEPS + TABLE_STEPS,
                           4: TAIL_STEPS + COMBINE_STEPS + TABLE_STEPS}
            for L in range(1, 5):
                per = CHUNK_STEPS[L]
                if L > 1:
                    Order.base, Order.n = total, 0
                    blocks_and_chunks(L, 0)
                    assert Order.n == FIRST_STEPS[L], (L, Order.n, FIRST_STEPS[L])
                    total += FIRST_STEPS[L]
                start = 1 if L > 1 else 0
                with dve.Fori(start, per_group) as s:
                    Order.base, Order.n = s * per + (total - start * per), 0
                    blocks_and_chunks(L, s)
                    assert Order.n == per, (L, Order.n, per)
                total += (per_group - start) * per
            for s in range(per_group):
                Order.base, Order.n = total, 0
                combine_choice(5, s, 0, s % 2, 3 * per_group + s // 2 + 1 if s % 2 == 0 else s // 2 + 1)
                combine_choice(5, s, 1, s % 2)
                combine_shared(5, s)
                total += COMBINE_STEPS


_INS = ['L0_attn_x', 'L0_attn_Wq', 'L0_attn_Wk', 'L0_attn_Wv', 'L0_attn_Wo', 'L0_ffn_gate_w', 'L0_ffn_gate_b',
        'L0_ffn_w1', 'L0_ffn_b1', 'L0_ffn_w2', 'L0_ffn_b2', 'L0_ffn_ws1', 'L0_ffn_bs1', 'L0_ffn_ws2', 'L0_ffn_bs2']


def kernel(**inputs):
    import numpy as _np
    import concourse.bacc as _bacc
    from concourse import mybir as _mybir
    from concourse.bass_utils import run_bass_kernel_spmd as _run

    nc = _bacc.Bacc("TRN2", target_bir_lowering=False, num_devices=1)
    arrays, args = {}, []
    for name in _INS:
        a = _np.ascontiguousarray(inputs[name])
        arrays[f"in_{name}_dram"] = a
        args.append(nc.dram_tensor(f"in_{name}_dram", a.shape, _mybir.dt.from_np(a.dtype), kind="ExternalInput").ap())
    shape = arrays["in_L0_attn_x_dram"].shape
    args.append(nc.dram_tensor("out_0_dram", shape, _mybir.dt.float32, kind="ExternalOutput").ap())
    macaron_block(nc, *args)
    r = _run(nc, [arrays], core_ids=[0])
    return r.results[0]["out_0_dram"]
```

```python
from contextlib import ExitStack

import numpy as np

import concourse.bass as bass
from concourse import mybir

F32 = mybir.dt.float32
BF16 = mybir.dt.bfloat16
I32 = mybir.dt.int32
ALU = mybir.AluOpType
ACT = mybir.ActivationFunctionType
AX = mybir.AxisListType

P = 128
HEAD = 8
EPS = 1e-5
BIG = 3.0e38

TILES = 8
HALF = TILES // 2
SEQS = TILES // 2
CHUNK = TILES * P
BT = 4
BLOCK = BT * P
STEPS = 8
RING = 4
AHEAD = 5
FREE = 12

HBANK = [0, 1, 2, 0, 1, 2, 0, 1, 2, 0, 1, 2, 0, 1, 2, 1]


def back(pattern, at):
    n = len(pattern)
    return next(d for d in range(1, n + 1) if pattern[(at - d) % n] == pattern[at % n])


def macaron_block(nc, x, wq, wk, wv, wo, gate_w, gate_b, w1, b1, w2, b2, ws1, bs1, ws2, bs2, out):
    batch, seq, dim = x.shape
    experts, _, hidden = w1.shape
    HC = hidden // P
    NX = experts + 1
    SH = experts
    tokens = batch * seq
    groups = 2
    chunks = tokens // CHUNK
    per_group = chunks // groups
    gtok = tokens // groups
    SHARED = gtok // BLOCK
    ROUTED = (2 * gtok - experts) // BLOCK + experts
    NB = per_group * STEPS
    ROUTED_AT = NB - ROUTED
    RT = ROUTED
    assert dim == P and seq == 2 * P and HC == 4
    assert SHARED <= ROUTED_AT < STEPS + AHEAD
    CAP = gtok + BLOCK
    DUMMY = experts * CAP
    SROW = DUMMY + BLOCK
    NR = SROW + gtok
    NE = 4 * NB + 8
    K2 = 2 * TILES
    W = 2 * P + 2
    LAST = 3
    UNUSED = 2 * gtok
    STORED = LAST * NB + STEPS
    assert ROUTED_AT >= STEPS
    E_BASE = float(np.exp(1.0))
    EXP_BASE = float(np.exp(1.0 / np.sqrt(HEAD)))

    with ExitStack() as ctx:
        def sb(name, shape, dt=F32):
            return ctx.enter_context(nc.sbuf_tensor(name, shape, dt))

        def sem(name):
            return ctx.enter_context(nc.semaphore(name))

        def psum(name, shape, dt=F32):
            return ctx.enter_context(nc.psum_tensor(name, shape, dt))

        xbuf = nc.dram_tensor("slots_in", [4 * NR, W], BF16, kind="Internal").ap()
        ybuf = [nc.dram_tensor(f"slots_out{g}", [NB * BLOCK, P], F32, kind="Internal").ap() for g in range(groups)]

        ytok = nc.dram_tensor("token_out", [UNUSED + RING * BLOCK, P], F32, kind="Internal").ap()

        X = sb("X", [P, chunks * TILES, P])
        w1h = sb("w1h", [P, NX, hidden], BF16)
        w1l = sb("w1l", [P, NX, hidden], BF16)
        w2h = sb("w2h", [P, NX, HC * P], BF16)
        w2l = sb("w2l", [P, NX, HC * P], BF16)
        b1row = sb("b1row", [NX * HC, P])
        b1t = sb("b1t", [P, NX * HC])
        b2row = sb("b2row", [NX, P])
        b2t = sb("b2t", [P, NX])
        wst = sb("wst", [P, 2, 2, hidden])
        watt = sb("watt", [P, 4, P])
        wqT = sb("wqT", [P, P])
        wkT = sb("wkT", [P, P])
        woT = sb("woT", [P, P])
        gw = sb("gw", [P, experts])
        gb = sb("gb", [P, experts])
        idf = sb("idf", [P, P])
        idb = sb("idb", [P, P], BF16)
        onesb = sb("onesb", [P, P], BF16)
        upper = sb("upper", [P, P], BF16)
        mask = sb("mask", [P, P])
        rev = sb("rev", [P, experts])
        ecap = sb("ecap", [P, experts])
        mhalf = sb("mhalf", [P, TILES])
        ebase = sb("ebase", [P, TILES])
        expbase = sb("expbase", [P, SEQS * HEAD])
        tri = sb("tri", [1, experts, experts])
        nidx = sb("nidx", [1, RT])
        zero = sb("zero", [P, BT, W], BF16)
        xin = sb("xin", [P, RING, BT, W], BF16)
        oid = sb("oid", [P, 2 * RING, BT], I32)
        idf32 = sb("idf32", [P, 2, BT])
        idhop = sb("idhop", [P, 2, BT])
        tokid = sb("tokid", [P, 2, TILES])
        xT = sb("xT", [P, RING, 2, BLOCK], BF16)
        g32 = sb("g32", [P, 2, HC, BLOCK])
        gh = sb("gh", [P, 2, HC, BLOCK], BF16)
        gl = sb("gl", [P, 2, HC, BLOCK], BF16)
        yT = sb("yT", [P, 2, BLOCK])
        yout = sb("yout", [P, RING, BT, P])
        etab = sb("etab", [1, NE], I32)
        rtab = sb("rtab", [1, NE], I32)
        st6 = sb("st6", [P, TILES, 6])
        mv = sb("mv", [P, TILES, 2])
        ve = sb("ve", [P, TILES])
        rstd = sb("rstd", [P, TILES])
        xn = sb("xn", [P, TILES, P])
        xnT = sb("xnT", [P, CHUNK])
        xhl = sb("xhl", [P, 2, TILES, W], BF16)
        lg = sb("lg", [P, TILES, experts])
        lg2 = sb("lg2", [P, TILES, experts])
        cand = sb("cand", [P, TILES, experts])
        m12 = sb("m12", [P, 2, TILES])
        first = sb("first", [P, TILES])
        oh = sb("oh", [P, 2, TILES, experts])
        assign = sb("assign", [P, TILES, experts], BF16)
        asum = sb("asum", [P, experts], BF16)
        arow = sb("arow", [P, experts])
        dlog = sb("dlog", [P, TILES])
        edl = sb("edl", [P, TILES])
        den = sb("den", [P, TILES])
        rden = sb("rden", [P, TILES])
        rk = sb("rk", [P, TILES, experts])
        pick = sb("pick", [P, 2, TILES, experts])
        idx = sb("idx", [P, 2, K2], I32)
        pos = sb("pos", [P, per_group, K2])
        posge = sb("posge", [P, per_group * K2, experts])
        shift = sb("shift", [P, per_group * K2])
        hop = sb("hop", [P, experts])
        gix = sb("gix", [P, chunks, K2], I32)
        gidx = sb("gidx", [P, 2, K2], I32)
        wts = sb("wts", [P, 2, chunks * TILES])
        yg = sb("yg", [P, 2, K2, P])
        ysh = sb("ysh", [P, TILES, P])
        gram = sb("gram", [P, SEQS, P])
        gA = sb("gA", [P, SEQS, P])
        gm = sb("gm", [P, SEQS, P])
        hd = sb("hd", [P, SEQS, HEAD])
        hd2 = sb("hd2", [P, SEQS, HEAD])
        hmx = sb("hmx", [P, SEQS])
        hex_ = sb("hex", [P, SEQS, HEAD])
        hsum = sb("hsum", [P, SEQS])
        hrec = sb("hrec", [P, SEQS])
        hp = sb("hp", [P, SEQS, HEAD])
        prob = sb("prob", [P, SEQS, P])
        cT = sb("cT", [P, SEQS, P])
        weff = sb("weff", [P, SEQS, P])
        cnt = sb("cnt", [P, experts])
        padf = sb("padf", [1, experts])
        padrow = sb("padrow", [1, experts], I32)
        cnt_i = sb("cnt_i", [P, experts], I32)
        nb_i = sb("nb_i", [P, experts], I32)
        nb = sb("nb", [P, experts])
        cumm = sb("cumm", [1, experts, experts])
        cum = sb("cum", [1, experts])
        le = sb("le", [1, RT, experts])
        le2 = sb("le2", [1, RT, experts])
        en = sb("en", [1, RT])
        cp = sb("cp", [1, RT])
        bi = sb("bi", [1, RT])
        ok = sb("ok", [1, RT])
        bo = sb("bo", [1, RT])
        ro = sb("ro", [1, RT])

        hps = [psum(f"hps{i}", [P, BLOCK]) for i in range(3)]
        ytps = psum("ytps", [P, BLOCK])
        yps = psum("yps", [P, BT, P])
        tps = psum("tps", [P, 2, BT, P], BF16)
        c0 = psum("c0", [P, HALF, P])
        c1 = psum("c1", [P, SEQS, P])

        xload = [sem(f"xload{i}") for i in range(per_group + 1)]
        wload = [sem(f"wload{i}") for i in range(2)]
        w_hi, w_lo = sem("w_hi"), sem("w_lo")
        aload = sem("aload")
        zeroed = sem("zeroed")
        const_ready, pool_order = sem("const_ready"), sem("pool_order")
        wT_ready, wT_sb = sem("wT_ready"), sem("wT_sb")
        zero_ready = sem("zero_ready")
        block_in = [sem(f"block_in{i}") for i in range(RING)]
        turned, xT_ready = sem("turned"), sem("xT_ready")
        up_done, gelu_done = sem("up_done"), sem("gelu_done")
        hi0_done, hi1_done, lo_done = sem("hi0_done"), sem("hi1_done"), sem("lo_done")
        down_done, yT_ready, y_turned, y_ready = sem("down_done"), sem("yT_ready"), sem("y_turned"), sem("y_ready")
        y_stored = [sem(f"y_stored{i}") for i in range(RING)]
        ids_kept, returned = sem("ids_kept"), [sem(f"returned{i}") for i in range(RING)]
        tokens_back = [[sem(f"tokens_back{i}_{ch}") for ch in range(2)] for i in range(2)]
        dve_order = sem("dve_order")
        var_ready, rstd_ready, xn_ready = sem("var_ready"), sem("rstd_ready"), sem("xn_ready")
        xn_turned, xnT_ready = sem("xn_turned"), sem("xnT_ready")
        split_hi, split_lo = sem("split_hi"), sem("split_lo")
        gate_done, assign_ready, rank_done = sem("gate_done"), sem("assign_ready"), sem("rank_done")
        dlog_ready, edl_ready, idx_ready = sem("dlog_ready"), sem("edl_ready"), sem("idx_ready")
        scattered, shared_stored = [[sem(f"{what}{i}") for i in range(2)] for what in ("scattered", "shared_stored")]
        sums_ready, count_done, table_ready, padded = sem("sums_ready"), sem("count_done"), sem("table_ready"), sem("padded")
        gidx_ready, gathered = sem("gidx_ready"), [[sem(f"gathered{i}_{ch}") for ch in range(2)] for i in range(2)]
        shared_back, combined = [sem(f"shared_back{i}") for i in range(2)], sem("combined")
        gram_done, gram_sb, a_done, a_sb = sem("gram_done"), sem("gram_sb"), sem("a_done"), sem("a_sb")
        scores_done, hd_ready, exp_ready, prob_ready = sem("scores_done"), sem("hd_ready"), sem("exp_ready"), sem("prob_ready")
        ct_done, ct_sb, weff_done, weff_sb = sem("ct_done"), sem("ct_sb"), sem("weff_done"), sem("weff_sb")
        att_done, att_added = sem("att_done"), sem("att_added")
        stored, passed = sem("stored"), sem("passed")

        x_v = x.rearrange("(c b) (p j) d -> c p b j d", b=SEQS, j=2)

        def norm_count(L, s, which):
            if L < 2:
                return s + L * per_group
            return s * 2 + (2 * per_group + (L - 2) * 2 * per_group + which)

        def plan(L, s):
            first = isinstance(s, int)
            if L == 1 and first:
                return dict(last_norm=0, last_turn=1, last_split=1, last_gate=2, last_expert=8, route=3, rank=4,
                            take_ranks=5, slots=5, weights=6, count=6, table=7, stats1=9, norm1=11, turn1=13,
                            split=14, gate=15)
            if L == 1:
                return dict(route=0, rank=2, stats1=1, take_ranks=2, slots=2, norm1=3, weights=4, turn1=5, gate=6,
                            split=10)
            if first:
                tail = dict(route=0, rank=1, take_ranks=2, slots=2, weights=5, count=3, table=3)
                if L == 4:
                    return dict(tail, weights=10)
                return dict(tail, combine0=5, combine1=6, combine2=7, stats0=7, norm0=8, gram=8, ga=9, scores=10,
                            turn0a=9, turn0b=10, soft1=10, soft2=12, ct=13, weff=13, out=13, stats1=13, norm1=14,
                            turn1=15, split=15, gate=15)
            if L == 4:
                return dict(combine0=1, combine1=4, combine2=4)
            return dict(route=0, rank=1, combine0=0, take_ranks=2, slots=5, combine1=1, combine2=3, stats0=3,
                        weights=6, norm0=4, gram=5, ga=6, scores=7, turn0a=7, turn0b=8, soft1=6, soft2=9, ct=10,
                        weff=11, out=12, stats1=12, norm1=13, turn1=14, split=14, gate=15)

        def shared_buffer(L, s):
            return s % 2 if L == 5 else 0

        def shared_rows(par):
            return wst[:, 0, :, :].rearrange("p a (b d) -> p (a b) d", d=P) if par else ysh[:, :, :]

        def combined_in(L, s):
            return s - 1 if L == 4 else s

        def tail_of(L, s):
            return (L - 1, per_group - 1) if isinstance(s, int) else (L, s - 1)

        def iterations(eng, L, body):
            body(L, 0)
            with eng.Fori(1, per_group) as s:
                body(L, s)

        def chunk_of(L, s):
            return s + (L % groups) * per_group

        def parity(L, s):
            return (s + 1) % 2 if L == 0 else 0

        def wait_apart(eng, sem, value):
            eng.wait_ge(sem, value)
            eng.sem_inc(passed, 1)

        def copies(L, s):
            return (0, 1) if L == LAST else (parity(L, s),)

        def row_ids(rows):
            return rows[:, :, 2 * P:W].bitcast(I32)[:, :, 0]

        def batch(s):
            return range(2 * s, 2 * s + 2)

        def look_up(eng, table, n, most):
            return nc.values_load(table[0:1, bass.ds(n, 1)], engines=[eng.engine], min_val=0, max_val=most,
                                  skip_runtime_bounds_check_because="the table is built from counts that bound its values")

        def first_buffer(L):
            return (L * per_group) - 2

        def buffer_free(eng, sems, per_stage, L, s):
            if L == 0:
                if s >= 2:
                    eng.wait_ge(sems[parity(L, s)], per_stage + (0 if parity(L, s) else 16))
            else:
                eng.wait_ge(sems[0], s * per_stage + (first_buffer(L) * per_stage + 16))

        block = ctx.enter_context(nc.Block())

        @block.sync
        def _(sp):
            for t in range(RING):
                sp.sem_inc(y_stored[t], 16)
            sp.sem_inc(turned, FREE)
            sp.sem_inc(shared_stored[0], 16)

            def load_x(c):
                sp.dma_start(X[:, c * TILES:(c + 1) * TILES, :].rearrange("p (b j) d -> p b j d", b=SEQS),
                             x_v[c]).then_inc(xload[min(c, per_group)], 16)

            def load_expert(n):
                e = SH if n == 0 else n - 1
                if n >= 2:
                    sp.wait_ge(w_lo, 2 * (n - 1))
                sp.dma_start(wst[:, n % 2, 0, :], ws1 if e == SH else w1[e]).then_inc(wload[n % 2], 16)
                sp.dma_start(wst[:, n % 2, 1, :].rearrange("p (j d) -> p j d", j=HC),
                             (ws2 if e == SH else w2[e]).rearrange("(j p) d -> p j d", p=P)).then_inc(wload[n % 2], 16)

            def store_shared(L, s):
                wait_apart(sp, split_lo, s + (L * per_group + 1))
                row = s * CHUNK + ((L * NR) + SROW)
                sp.dma_start(xbuf[bass.ds(row, CHUNK), :].rearrange("(p t) d -> p t d", t=TILES),
                             xhl[:, parity(L, s), :, :]).then_inc(shared_stored[parity(L, s)], 16)

            def load_block(n, slot, kept=None):
                if not isinstance(n, int) or n >= RING:
                    wait_apart(sp, turned, n + (FREE - RING + 1))
                if kept is not None:
                    wait_apart(sp, ids_kept, kept)
                row = look_up(sp, rtab, n, 4 * NR - BLOCK)
                sp.dma_start(xin[:, slot, :, :], xbuf[bass.ds(row, BLOCK), :].rearrange("(p j) d -> p j d", j=BT))\
                    .then_inc(block_in[slot], 16)

            def store_block(L, s, u):
                n = s * STEPS + ((L - 1) * NB + u)
                wait_apart(sp, y_ready, n + (1 + FREE))
                row = s * (STEPS * BLOCK) + u * BLOCK
                sp.dma_start(ybuf[(L - 1) % groups][bass.ds(row, BLOCK), :].rearrange("(p j) d -> p j d", j=BT),
                             yout[:, u % RING, :, :]).then_inc(y_stored[u % RING], 16)

            def pad_slots(L):
                sp.wait_ge(table_ready, L + 1)
                for e in range(experts):
                    row = look_up(sp, padrow, e, 4 * NR - BLOCK)
                    sp.dma_start(xbuf[bass.ds(row, BLOCK), :].rearrange("(p j) d -> p j d", j=BT), zero[:, :, :])\
                        .then_inc(padded, 16)
                sp.wait_ge(padded, 16 * experts * (L + 1))

            def fetch_shared(L, s):
                par = shared_buffer(L, s)
                if not (L == 5 and s == 1):
                    wait_apart(sp, combined, s + ((L - 2) * per_group + FREE - (1 if L == 5 and s > 1 else 0)))
                sp.dma_start(shared_rows(par), ybuf[L % groups][bass.ds(s * CHUNK, CHUNK), :].rearrange("(p t) d -> p t d", t=TILES))\
                    .then_inc(shared_back[par], 16)

            def fetch_tokens(s):
                for k in range(2):
                    row = k * gtok + s * CHUNK
                    sp.dma_start(yg[:, s % 2, k * TILES:(k + 1) * TILES, :],
                                 ytok[row:row + CHUNK, :].rearrange("(p t) d -> p t d", t=TILES))\
                        .then_inc(tokens_back[s % 2][k], 16)

            def store_chunk(L, s):
                c = chunk_of(L, s)
                wait_apart(sp, combined, s + ((L - 2) * per_group + FREE + 1))
                for b in range(SEQS):
                    src = X[:, bass.ds(c * TILES + 2 * b, 2), :]
                    dst = out[bass.ds(c * SEQS + b, 1)].rearrange("a (p j) d -> (a p) j d", j=2)
                    sp.dma_start(dst, src).then_inc(stored, 16)

            for c in range(per_group):
                load_x(c)
                if c == 0:
                    for n, w in enumerate((wq, wk, wv, wo)):
                        sp.dma_start(watt[:, n, :], w).then_inc(aload, 16)
                    sp.dma_start(gw[:, :], gate_w).then_inc(aload, 16)
                    sp.dma_start(gb[:, :], gate_b.rearrange("(a e) -> a e", a=1).to_broadcast([P, experts])).then_inc(aload, 16)
                    sp.dma_start(b1row[0:experts * HC, :], b1.rearrange("e (j p) -> (e j) p", p=P)).then_inc(aload, 16)
                    sp.dma_start(b1row[experts * HC:NX * HC, :], bs1.rearrange("(j p) -> j p", p=P)).then_inc(aload, 16)
                    sp.dma_start(b2row[0:experts, :], b2).then_inc(aload, 16)
                    sp.dma_start(b2row[experts:NX, :], bs2.rearrange("(a d) -> a d", a=1)).then_inc(aload, 16)
            load_expert(0)
            load_expert(1)
            for c in range(per_group, chunks):
                load_x(c)
            sp.wait_ge(const_ready, 1)
            for g in range(1, 4):
                sp.dma_start(xbuf[g * NR + DUMMY:g * NR + DUMMY + BLOCK, :].rearrange("(p j) d -> p j d", j=BT),
                             zero[:, :, :]).then_inc(zero_ready, 16)
            for s in range(per_group - 1):
                store_shared(0, s)
                for n in batch(s):
                    if n + 2 < NX:
                        load_expert(n + 2)
                if s == 1:
                    for i in range(2):
                        sp.wait_ge(shared_stored[i], 16 + (0 if i else 16))
                    sp.wait_ge(const_ready, 2)
                    for n in range(RING):
                        load_block(n, n)
            sp.wait_ge(zero_ready, 48)
            sp.wait_ge(scattered[0], 16)
            sp.wait_ge(shared_stored[1], 32)
            for n in range(RING, AHEAD):
                load_block(n, n % RING)

            def blocks_and_chunks(L, s):
                first = isinstance(s, int)
                if L < 4 and not (L == 1 and first):
                    wait_apart(sp, shared_stored[0], s * 16 + (16 * (first_buffer(L) + 1)))
                if L in (2, 3) and not first:
                    fetch_shared(L, s)
                for u in range(STEPS):
                    n = s * STEPS + ((L - 1) * NB + u)
                    if L >= 2 and first and u == 1:
                        for t in range(RING):
                            sp.wait_ge(y_stored[t], 16 * (NB // RING * (L - 1) + 1 + (t < u)))
                        fetch_shared(L, s)
                    if L == 1 and first and n + AHEAD == (SHARED // per_group) * (per_group - 1):
                        store_shared(0, per_group - 1)
                        load_expert(NX - 1)
                        sp.wait_ge(shared_stored[0], 32 + 16)
                    if u + AHEAD == ROUTED_AT:
                        if first:
                            pad_slots(L - 1)
                            sp.wait_ge(scattered[0], 16 * K2 * first_buffer(L) + 16)
                            sp.wait_ge(scattered[1], 2 * 16 * K2)
                    if L == 4 and not first and u == 2:
                        store_chunk(L, s - 1)
                        fetch_shared(L, s)
                    kept = None
                    if L == LAST + 1 and (not first or u + AHEAD - RING >= STEPS):
                        kept = (s - 1) * STEPS + (u + AHEAD - RING + 1)
                    load_block(n + AHEAD, (u + AHEAD) % RING, kept)
                    if L < LAST + 1 or first:
                        store_block(L, s, u)
                if L < 4:
                    store_shared(L, s)

            for L in range(1, 5):
                iterations(sp, L, blocks_and_chunks)

            for t in range(RING):
                sp.wait_ge(returned[t], 16 + 16 * BT * (per_group - 1) * STEPS // RING)
            for s in range(per_group):
                if s == 1:
                    store_chunk(4, per_group - 1)
                if s >= 2:
                    store_chunk(5, s - 2)
                fetch_tokens(s)
                fetch_shared(5, s)
            for s in range(per_group - 2, per_group):
                store_chunk(5, s)
            sp.wait_ge(stored, 16 * SEQS * chunks)
            for t in range(RING):
                sp.wait_ge(y_stored[t], 16 * (STORED // RING + 1))
            for t in range(RING):
                sp.wait_ge(block_in[t], 16 * (NB // RING * 4 + 1 + (t < AHEAD - RING)))

        @block.gpsimd
        def _(pool):
            pool.memset(zero[:, :, :], 0.0).then_inc(zeroed, 1)
            pool.wait_ge(zeroed, 1)
            pool.iota(row_ids(zero), [[1, BT]], base=UNUSED, channel_multiplier=BT).then_inc(const_ready, 1)
            order = [0]

            def put(inst):
                order[0] += 1
                inst.then_inc(pool_order, 1)
            put(pool.memset(mhalf[:, :], -0.5))
            put(pool.memset(ebase[:, :], E_BASE))
            put(pool.memset(idf[:, :], 0.0))
            put(pool.memset(idb[:, :], 0.0))
            put(pool.memset(etab[:, :], SH))
            put(pool.memset(onesb[:, :], 1.0))
            put(pool.memset(upper[:, :], 0.0))
            put(pool.memset(mask[:, :], 1.0))
            put(pool.memset(tri[:, :, :], 1.0))
            put(pool.memset(expbase[:, :], EXP_BASE))
            put(pool.memset(asum[:, :], 0.0))
            put(pool.memset(rtab[:, :], DUMMY))
            put(pool.iota(rev[:, :], [[-1, experts]], base=experts, channel_multiplier=0, allow_small_or_imprecise_dtypes=True))
            put(pool.iota(ecap[:, :], [[CAP, experts]], base=0, channel_multiplier=0, allow_small_or_imprecise_dtypes=True))
            put(pool.iota(nidx[:, :], [[1, RT]], base=0, channel_multiplier=0, allow_small_or_imprecise_dtypes=True))
            put(pool.iota(tokid[:, :, :], [[gtok, 2], [1, TILES]], base=0, channel_multiplier=TILES,
                          allow_small_or_imprecise_dtypes=True))
            pool.wait_ge(pool_order, order[0])
            for g in range(4):
                put(pool.iota(rtab[:, g * NB:g * NB + SHARED], [[BLOCK, SHARED]], base=g * NR + SROW, channel_multiplier=0))
            for m in (idf, idb):
                put(pool.affine_select(out=m[:, :], in_=m[:, :], compare_op=ALU.not_equal, fill=1.0, base=0,
                                       pattern=[[-1, P]], channel_multiplier=1))
            put(pool.affine_select(out=upper[:, :], in_=upper[:, :], compare_op=ALU.is_ge, fill=1.0, base=0,
                                   pattern=[[-1, P]], channel_multiplier=1))
            put(pool.affine_select(out=tri[:, :, :], in_=tri[:, :, :], compare_op=ALU.is_ge, fill=0.0, base=0,
                                   pattern=[[1, experts], [-1, experts]], channel_multiplier=0))
            mk = mask[:, :].rearrange("p (k i) -> p k i", i=HEAD)
            put(pool.affine_select(out=mk, in_=mk, compare_op=ALU.is_ge, fill=0.0, base=0,
                                   pattern=[[-HEAD, P // HEAD], [0, HEAD]], channel_multiplier=1))
            pool.wait_ge(pool_order, order[0])
            pool.affine_select(out=mk, in_=mk, compare_op=ALU.is_ge, fill=0.0, base=HEAD - 1,
                               pattern=[[HEAD, P // HEAD], [0, HEAD]], channel_multiplier=-1).then_inc(const_ready, 1)
            pool.dma_start(xbuf[DUMMY:DUMMY + BLOCK, :].rearrange("(p j) d -> p j d", j=BT), zero[:, :, :]).then_inc(scattered[0], 16)
            pool.sem_inc(combined, FREE)

            def root(n):
                pool.wait_ge(var_ready, n + 1)
                pool.tensor_tensor(rstd[:, :], ve[:, :], mhalf[:, :], ALU.pow).then_inc(rstd_ready, 1)

            def gate_exp(r):
                pool.wait_ge(dlog_ready, r + 1)
                pool.tensor_tensor(edl[:, :], ebase[:, :], dlog[:, :], ALU.pow).then_inc(edl_ready, 1)

            def head_exp(t):
                pool.wait_ge(hd_ready, t + 1)
                pool.tensor_tensor(hex_[:, :, :], expbase[:, :].rearrange("p (b i) -> p b i", b=SEQS), hd2[:, :, :], ALU.pow)\
                    .then_inc(exp_ready, 1)

            def scatter(r, par, rows=range(K2), both=False):
                if rows[0] == 0:
                    pool.wait_ge(split_lo, r + 1)
                    wait_apart(pool, idx_ready, r + 1)
                for a in rows:
                    pool.indirect_dma_start(xbuf[:, :], bass.IndirectOffsetOnAxis(idx[:, par, a:a + 1], 0),
                                            xhl[:, a // TILES if both else par, a % TILES, :], None)\
                        .then_inc(scattered[par], 16)

            def gather(L, s, par=0, rows=range(K2)):
                k = s + (L - 2) * per_group
                c = chunk_of(L, s)
                if rows[0] == 0:
                    if par == 0:
                        pool.wait_ge(combined, k + FREE)
                    pool.tensor_copy(gidx[:, par, :], gix[:, bass.ds(c, 1), :].rearrange("p a k -> p (a k)"))\
                        .then_inc(gidx_ready, 1)
                    before = k if L < 4 or isinstance(s, int) and s == 0 else 2 * per_group + 1 if par else k + 1
                    wait_apart(pool, gidx_ready, before + 1)
                for a in rows:
                    pool.indirect_dma_start(yg[:, par, a, :], None, ybuf[L % groups][:, :],
                                            bass.IndirectOffsetOnAxis(gidx[:, par, a:a + 1], 0))\
                        .then_inc(gathered[par][a // TILES], 16)

            root(norm_count(0, 0, 1))
            for t in range(RING):
                pool.dma_start(ytok[UNUSED + t:UNUSED + t + 1, 0:TILES], mhalf[t:t + 1, :]).then_inc(returned[t], 16)
            for s in range(per_group - 1):
                gate_exp(s)
                root(norm_count(0, s + 1, 1))
                scatter(s, parity(0, s))
            gate_exp(per_group - 1)
            scatter(per_group - 1, 0)
            root(norm_count(1, 0, 1))
            with pool.Fori(1, per_group) as s:
                gate_exp(s + (per_group - 1))
                root(norm_count(1, s, 1))
                scatter(s + (per_group - 1), 0)

            def part(a, b):
                return range(a * K2 // 8, b * K2 // 8)

            def outputs_stored(L):
                pool.wait_ge(table_ready, L - 1)
                for t in range(RING):
                    pool.wait_ge(y_stored[t], 16 * (NB // RING * (L - 1) + 1))

            for L in range(2, 4):
                outputs_stored(L)
                gather(L, 0)
                gate_exp(L * per_group - 1)
                scatter(L * per_group - 1, 0, part(0, 1))
                root(norm_count(L, 0, 0))
                scatter(L * per_group - 1, 0, part(1, 8))
                head_exp((L - 2) * per_group)
                gather(L, 1, 0, part(0, 1))
                root(norm_count(L, 0, 1))
                gather(L, 1, 0, part(1, 8))

                def rest(s, last):
                    r = s + (L * per_group - 1)
                    gate_exp(r)
                    root(norm_count(L, s, 0))
                    scatter(r, 0, part(0, 4), L == LAST)
                    head_exp(s + (L - 2) * per_group)
                    scatter(r, 0, part(4, 8), L == LAST)
                    if not last:
                        gather(L, s + 1, 0, part(0, 3))
                    root(norm_count(L, s, 1))
                    if not last:
                        gather(L, s + 1, 0, part(3, 8))
                with pool.Fori(1, per_group - 1) as s:
                    rest(s, False)
                rest(per_group - 1, True)

            def return_block(n, u):
                wait_apart(pool, ids_kept, n - (LAST * NB + STEPS - 1))
                wait_apart(pool, y_ready, n + (1 + FREE))
                for j in range(BT):
                    pool.indirect_dma_start(ytok[:, :], bass.IndirectOffsetOnAxis(oid[:, u % (2 * RING), j:j + 1], 0),
                                            yout[:, u % RING, j, :], None).then_inc(returned[u % RING], 16)

            scatter(4 * per_group - 1, 0, both=True)
            gate_exp(4 * per_group - 1)
            outputs_stored(4)
            gather(4, 0)
            gather(4, per_group - 1, 1)

            def return_blocks(s, last):
                for u in range(STEPS):
                    return_block(s * STEPS + (LAST * NB + u), u)
                    if not last and u >= 3:
                        at = range(K2)[(u - 3) * K2 // (STEPS - 3):(u - 2) * K2 // (STEPS - 3)]
                        gather(4, s, 0, at)

            with pool.Fori(1, per_group - 1) as s:
                return_blocks(s, False)
            return_blocks(per_group - 1, True)
            for t in range(RING):
                pool.wait_ge(returned[t], 16 + 16 * BT * (per_group - 1) * STEPS // RING)
            pool.wait_ge(scattered[0], 16 + 16 * K2 * first_buffer(4))

        @block.tensor
        def _(pe):
            pe.wait_ge(aload, 160)
            pe.wait_ge(const_ready, 2)
            for n, m in enumerate((0, 1, 3)):
                pe.transpose(c0[:, n, :], watt[:, m, :], idf[:, :])
            pe.transpose(c0[:, 3, 0:NX * HC], b1row[:, :], idf[0:NX * HC, 0:NX * HC])
            pe.transpose(c0[:, 3, NX * HC:NX * HC + NX], b2row[:, :], idf[0:NX, 0:NX]).then_inc(wT_ready, 1)
            pe.wait_ge(wT_sb, 5)

            def turn_half(n, h, bank=None):
                pe.wait_ge(xn_ready, n + 1)
                if h == 1 and bank is None:
                    pe.wait_ge(xnT_ready, n * 2 + 1)
                for t in range(HALF):
                    last = pe.transpose((bank or c0)[:, t, :], xn[:, h * HALF + t, :], idf[:, :])
                last.then_inc(xn_turned, 1)

            def turn_both(n):
                turn_half(n, 0)
                turn_half(n, 1, c1)

            def gate(n, r):
                pe.wait_ge(xnT_ready, n * 2 + 2)
                for t in range(TILES):
                    last = pe.matmul(c1[:, 0, t * experts:(t + 1) * experts], xnT[:, t * P:(t + 1) * P], gw[:, :],
                                     start=True, stop=True)
                last.then_inc(gate_done, 1)

            def rank(r):
                pe.wait_ge(assign_ready, r + 1)
                o = c1[:, 0, 0:TILES * experts].rearrange("p (t e) -> p t e", t=TILES)
                pe.matmul(o, upper[:, :], assign[:, :, :], start=True, stop=False)
                pe.matmul(o, onesb[:, :], asum[:, :].unsqueeze(1).to_broadcast([P, TILES, experts]), start=False, stop=False)
                for t in range(1, TILES):
                    last = pe.matmul(o[:, t:, :], onesb[:, :], assign[:, 0:TILES - t, :], start=False, stop=t == TILES - 1)
                last.then_inc(rank_done, 1)

            def count(L):
                pe.wait_ge(sums_ready, L + 1)
                pe.matmul(c1[:, 0, 0:experts], onesb[:, :], asum[:, :], start=True, stop=True).then_inc(count_done, 1)

            def att_gram(n, t):
                pe.wait_ge(xn_ready, n + 1)
                for b in range(SEQS):
                    for j in range(2):
                        v = xn[:, 2 * b + j, :]
                        last = pe.matmul(c1[:, b, :], v, v, start=j == 0, stop=j == 1)
                last.then_inc(gram_done, 1)

            def att_product(ready, t, lhsT, rhs, done):
                pe.wait_ge(ready, t + 1)
                for b in range(SEQS):
                    last = pe.matmul(c1[:, b, :], lhsT[:, b, :], rhs, start=True, stop=True)
                last.then_inc(done, 1)

            def att_out(n, t):
                pe.wait_ge(weff_sb, t + 1)
                pe.wait_ge(xnT_ready, n * 2 + 2)
                for h, bank in enumerate((c0, c1)):
                    for a in range(HALF):
                        tile = h * HALF + a
                        last = pe.matmul(bank[:, a, :], xnT[:, tile * P:(tile + 1) * P], weff[:, tile // 2, :],
                                         start=True, stop=True)
                    last.then_inc(att_done, 1)

            def turn_block(n, slot, landed):
                pe.wait_ge(block_in[slot], landed)
                pe.wait_ge(xT_ready, n + FREE)
                for h in range(2):
                    for j in range(BT):
                        last = pe.transpose(tps[:, h, j, :], xin[:, slot, j, h * P:(h + 1) * P], idb[:, :])
                last.then_inc(turned, 1)

            def up(n, u, e):
                slot = u % RING
                pe.wait_ge(xT_ready, n + FREE + 1)
                for j in range(HC):
                    at = HC * slot + j
                    bank = hps[HBANK[at]]
                    pe.wait_ge(gelu_done, n * HC + (j + 1 - back(HBANK, at) + FREE))
                    wh = w1h[:, bass.ds(e, 1), j * P:(j + 1) * P].rearrange("p a d -> p (a d)")
                    wl = w1l[:, bass.ds(e, 1), j * P:(j + 1) * P].rearrange("p a d -> p (a d)")
                    pe.matmul(bank[:, :], wh, xT[:, slot, 0, :], start=True, stop=False)
                    pe.matmul(bank[:, :], wh, xT[:, slot, 1, :], start=False, stop=False)
                    pe.matmul(bank[:, :], wl, xT[:, slot, 0, :], start=False, stop=True).then_inc(up_done, 1)

            def turn_y(n, u):
                pe.wait_ge(yT_ready, n + (1 + FREE))
                pe.wait_ge(y_ready, n + FREE)
                for t in range(BT):
                    last = pe.transpose(yps[:, t, :], yT[:, u % 2, t * P:(t + 1) * P], idf[:, :])
                last.then_inc(y_turned, 1)

            def down(n, u, e):
                g = u % 2
                pe.wait_ge(yT_ready, n + FREE)
                for j in range(HC):
                    if j == 0:
                        pe.wait_ge(hi0_done, n + 1)
                        pe.wait_ge(lo_done, n * 2 + 1)
                    if j == HC // 2:
                        pe.wait_ge(lo_done, n * 2 + 2)
                    wh = w2h[:, bass.ds(e, 1), j * P:(j + 1) * P].rearrange("p a d -> p (a d)")
                    wl = w2l[:, bass.ds(e, 1), j * P:(j + 1) * P].rearrange("p a d -> p (a d)")
                    pe.matmul(ytps[:, :], wh, gh[:, g, j, :], start=j == 0, stop=False)
                    pe.matmul(ytps[:, :], wh, gl[:, g, j, :], start=False, stop=False)
                    last = pe.matmul(ytps[:, :], wl, gh[:, g, j, :], start=False, stop=j == HC - 1)
                last.then_inc(down_done, 1)

            pe.sem_inc(down_done, FREE)
            for s in range(per_group - 1):
                n1 = norm_count(0, s, 1)
                turn_both(n1)
                if s == 2:
                    turn_block(2, 2, 16)
                    up(1, 1, SH)
                gate(n1, s)
                if s == 2:
                    down(0, 0, SH)
                rank(s)
                if s == 1:
                    pe.wait_ge(w_lo, 2)
                    turn_block(0, 0, 16)
                    turn_block(1, 1, 16)
                    up(0, 0, SH)

            def blocks_and_chunks(L, s):
                first = isinstance(s, int)
                n0 = norm_count(L, s, 0)
                n1 = norm_count(L, s, 1)
                t_ = s + (L - 2) * per_group
                Lt, st = tail_of(L, s)
                n_last = norm_count(0, per_group - 1, 1)
                at = plan(L, s)

                def chunk_part(h):
                    if at.get("last_turn") == h:
                        turn_both(n_last)
                    if at.get("last_gate") == h:
                        gate(n_last, per_group - 1)
                    if at.get("rank") == h:
                        rank(st + Lt * per_group)
                    if at.get("count") == h:
                        count(L - 1)
                    if at.get("gram") == h:
                        att_gram(n0, t_)
                    if at.get("turn0a") == h:
                        turn_half(n0, 0)
                    if at.get("ga") == h:
                        att_product(gram_sb, t_, gram, wkT[:, :], a_done)
                    if at.get("turn0b") == h:
                        turn_half(n0, 1)
                    if at.get("scores") == h:
                        att_product(a_sb, t_, gA, wqT[:, :], scores_done)
                    if at.get("ct") == h:
                        att_product(prob_ready, t_, prob, watt[:, 2, :], ct_done)
                    if at.get("weff") == h:
                        att_product(ct_sb, t_, cT, woT[:, :], weff_done)
                    if at.get("out") == h:
                        att_out(n0, t_)
                    if at.get("turn1") == h:
                        turn_both(n1)
                    if at.get("gate") == h:
                        gate(n1, s + L * per_group)

                e_next = look_up(pe, etab, s * STEPS + ((L - 1) * NB + 1), SH)
                for u in range(STEPS):
                    n = s * STEPS + ((L - 1) * NB + u)
                    if u == ROUTED_AT - 2 and first:
                        pe.wait_ge(table_ready, L)
                        if L == 1:
                            pe.wait_ge(w_lo, 2 * NX)
                    e_down, e_next = e_next, look_up(pe, etab, n + 2, SH)
                    turn_block(n + 3, (u + 3) % RING, s * (16 * STEPS // RING) + 16 * ((L - 1) * NB // RING + (u + 3) // RING + 1))
                    up(n + 2, u + 2, e_next)
                    chunk_part(2 * u)
                    turn_y(n, u)
                    down(n + 1, u + 1, e_down)
                    chunk_part(2 * u + 1)

            for L in range(1, 5):
                iterations(pe, L, blocks_and_chunks)

        @block.scalar
        def _(act):
            act.wait_ge(wT_ready, 1)
            for n, m in enumerate((wqT, wkT, woT)):
                act.activation(m[:, :], c0[:, n, :], ACT.Copy).then_inc(wT_sb, 1)
            act.activation(b1t[:, :], c0[:, 3, 0:NX * HC], ACT.Copy).then_inc(wT_sb, 1)
            act.activation(b2t[:, :], c0[:, 3, NX * HC:NX * HC + NX], ACT.Copy).then_inc(wT_sb, 1)

            def weights_high(n):
                e = SH if n == 0 else n - 1
                act.wait_ge(wload[n % 2], 32 * (n // 2 + 1))
                act.activation(w1h[:, e, :], wst[:, n % 2, 0, :], ACT.Copy).then_inc(w_hi, 1)
                act.activation(w2h[:, e, :], wst[:, n % 2, 1, :], ACT.Copy).then_inc(w_hi, 1)

            def split_high(L, s):
                act.wait_ge(xn_ready, norm_count(L, s, 1) + 1)
                buffer_free(act, scattered, 16 * K2, L, s)
                buffer_free(act, shared_stored, 16, L, s)
                for k in copies(L, s):
                    last = act.activation(xhl[:, k, :, 0:P], xn[:, :, :], ACT.Copy)
                last.then_inc(split_hi, 1)

            def take_xnT(n, h, bank=None):
                act.wait_ge(xn_turned, n * 2 + (h + 2))
                act.activation(xnT[:, h * HALF * P:(h + 1) * HALF * P], (bank or c0)[:, :, :].rearrange("p t d -> p (t d)"), ACT.Copy)\
                    .then_inc(xnT_ready, 1)

            def take(done, t, dst, kept):
                act.wait_ge(done, t + 1)
                act.activation(dst[:, :, :], c1[:, :, :], ACT.Copy).then_inc(kept, 1)

            def gelus(n, u, js, e):
                slot = u % RING
                for j in js:
                    act.wait_ge(up_done, n * HC + (j + 1))
                    if j == 0:
                        act.wait_ge(down_done, n + (FREE - 1))
                    act.activation(g32[:, u % 2, j, :], hps[HBANK[HC * slot + j]][:, :], ACT.Gelu,
                                   bias=b1t[:, bass.ds(e * HC + j, 1)]).then_inc(gelu_done, 1)

            def high(n, u, half):
                act.wait_ge(gelu_done, n * HC + (2 * half + 2 + FREE))
                act.activation(gh[:, u % 2, 2 * half:2 * half + 2, :], g32[:, u % 2, 2 * half:2 * half + 2, :], ACT.Copy)\
                    .then_inc((hi0_done, hi1_done)[half], 1)

            def take_yT(n, u, e):
                act.wait_ge(down_done, n + (1 + FREE))
                act.wait_ge(y_turned, n + (FREE - 1))
                act.activation(yT[:, u % 2, :], ytps[:, :], ACT.Identity, bias=b2t[:, bass.ds(e, 1)]).then_inc(yT_ready, 1)

            def take_y(n, u, left, before):
                act.wait_ge(y_turned, n + (1 + FREE))
                act.wait_ge(left[u % RING], before)
                act.activation(yout[:, u % RING, :, :], yps[:, :, :], ACT.Copy).then_inc(y_ready, 1)

            def hidden_values(n):
                gelus(n, n, (0, 1), SH)
                high(n, n, 0)
                gelus(n, n, (2, 3), SH)
                high(n, n, 1)

            act.sem_inc(xn_turned, 1)
            act.sem_inc(gelu_done, FREE)
            act.sem_inc(y_ready, FREE)
            act.sem_inc(yT_ready, FREE)
            act.sem_inc(y_turned, FREE)
            for s in range(per_group - 1):
                split_high(0, s)
                take_xnT(norm_count(0, s, 1), 0)
                take_xnT(norm_count(0, s, 1), 1, c1)
                for n in batch(s):
                    weights_high(n)
                if s >= 1:
                    hidden_values(s - 1)
            take_yT(0, 0, SH)

            def blocks_and_chunks(L, s):
                first = isinstance(s, int)
                n0 = norm_count(L, s, 0)
                n1 = norm_count(L, s, 1)
                t_ = s + (L - 2) * per_group
                n_last = norm_count(0, per_group - 1, 1)
                at = plan(L, s)

                def chunk_part(h):
                    if at.get("last_turn") == h:
                        take_xnT(n_last, 0)
                        take_xnT(n_last, 1, c1)
                    if at.get("last_split") == h:
                        split_high(0, per_group - 1)
                        for n in batch(per_group - 1):
                            weights_high(n)
                    if at.get("last_expert") == h:
                        weights_high(NX - 1)
                    if at.get("gram") == h:
                        take(gram_done, t_, gram, gram_sb)
                    if at.get("turn0a") == h:
                        take_xnT(n0, 0)
                    if at.get("ga") == h:
                        take(a_done, t_, gA, a_sb)
                    if at.get("turn0b") == h:
                        take_xnT(n0, 1)
                    if at.get("ct") == h:
                        take(ct_done, t_, cT, ct_sb)
                    if at.get("weff") == h:
                        take(weff_done, t_, weff, weff_sb)
                    if at.get("turn1") == h:
                        take_xnT(n1, 0)
                        take_xnT(n1, 1, c1)
                    if at.get("split") == h:
                        split_high(L, s)

                e_next = look_up(act, etab, s * STEPS + ((L - 1) * NB + 1), SH)
                for u in range(STEPS):
                    n = s * STEPS + ((L - 1) * NB + u)
                    if u == ROUTED_AT - 2 and first:
                        act.wait_ge(table_ready, L)
                    e_down, e_next = e_next, look_up(act, etab, n + 2, SH)
                    gelus(n + 2, u + 2, (0, 1), e_next)
                    high(n + 2, u + 2, 0)
                    gelus(n + 2, u + 2, (2, 3), e_next)
                    high(n + 2, u + 2, 1)
                    chunk_part(2 * u)
                    if L < LAST + 1 or first:
                        take_y(n, u, y_stored, s * (16 * STEPS // RING) + 16 * ((L - 1) * NB // RING + u // RING + 1))
                    else:
                        act.wait_ge(y_stored[u % RING], 16 * (STORED // RING + 1))
                        take_y(n, u, returned, (s - 1) * (16 * BT * STEPS // RING) + (16 * BT * (u // RING) + 16))
                    take_yT(n + 1, u + 1, e_down)
                    chunk_part(2 * u + 1)

            for L in range(1, 5):
                iterations(act, L, blocks_and_chunks)

        @block.vector
        def _(dve):
            class Order:
                base, n = 0, 0

            def step(inst):
                Order.n += 1
                inst.then_inc(dve_order, 1)

            def settle():
                dve.wait_ge(dve_order, Order.base + Order.n)

            def weights_low(n):
                e = SH if n == 0 else n - 1
                dve.wait_ge(w_hi, 2 * n + 2)
                dve.tensor_tensor(w1l[:, e, :], wst[:, n % 2, 0, :], w1h[:, e, :], ALU.subtract).then_inc(w_lo, 1)
                dve.tensor_tensor(w2l[:, e, :], wst[:, n % 2, 1, :], w2h[:, e, :], ALU.subtract).then_inc(w_lo, 1)

            def tile_of(c, t):
                return X[:, bass.ds(c * TILES + t, 1), :].rearrange("p a d -> p (a d)")

            def stats(c, n):
                for t in range(TILES):
                    step(dve.bn_stats(st6[:, t, :], tile_of(c, t)))
                wait_apart(dve, dve_order, Order.base + Order.n)
                for t in range(TILES):
                    step(dve.bn_aggr(mv[:, t, :], st6[:, t, :]))
                settle()
                dve.tensor_scalar(ve[:, :], mv[:, :, 1], EPS, None, ALU.add).then_inc(var_ready, 1)

            def normalise(c, n):
                dve.wait_ge(rstd_ready, n + 1)
                dve.wait_ge(xn_turned, n * 2 + 1)
                for t in range(TILES):
                    last = dve.tensor_scalar(xn[:, t, :], tile_of(c, t),
                                             mv[:, t, 0:1], rstd[:, t:t + 1], ALU.subtract, ALU.mult)
                last.then_inc(xn_ready, 1)

            def split_low(L, s):
                dve.wait_ge(split_hi, s + (L * per_group + 1))
                if L == LAST:
                    for k in copies(L, s):
                        step(dve.tensor_scalar(row_ids(xhl[:, k, :, :]), tokid[:, k, :], 0.0, None, ALU.add))
                    settle()
                    step(dve.tensor_scalar(tokid[:, :, :], tokid[:, :, :], float(CHUNK), None, ALU.add))
                for k in copies(L, s):
                    last = dve.tensor_tensor(xhl[:, k, :, P:2 * P], xn[:, :, :], xhl[:, k, :, 0:P], ALU.subtract)
                last.then_inc(split_lo, 1)

            def over_e(ap):
                return ap.unsqueeze(2).to_broadcast([P, TILES, experts])

            def over_t(ap):
                return ap.unsqueeze(1).to_broadcast([P, TILES, experts])

            def choose(k, src):
                step(dve.reduce_max(m12[:, k, :], src, AX.X))
                settle()
                step(dve.tensor_tensor(cand[:, :, :], src, over_e(m12[:, k, :]), ALU.is_ge))
                settle()
                step(dve.tensor_tensor(cand[:, :, :], cand[:, :, :], over_t(rev[:, :]), ALU.mult))
                settle()
                step(dve.reduce_max(first[:, :], cand[:, :, :], AX.X))
                settle()
                step(dve.tensor_tensor(oh[:, k, :, :], over_t(rev[:, :]), over_e(first[:, :]), ALU.is_equal))
                settle()

            def route(L, s):
                dve.wait_ge(gate_done, s + (L * per_group + 1))
                step(dve.tensor_tensor(lg[:, :, :], c1[:, 0, 0:TILES * experts].rearrange("p (t e) -> p t e", t=TILES),
                                       over_t(gb[:, :]), ALU.add))
                settle()
                choose(0, lg[:, :, :])
                step(dve.scalar_tensor_tensor(lg2[:, :, :], oh[:, 0, :, :], -BIG, lg[:, :, :], ALU.mult, ALU.add))
                settle()
                choose(1, lg2[:, :, :])
                dve.tensor_tensor(assign[:, :, :], oh[:, 0, :, :], oh[:, 1, :, :], ALU.add).then_inc(assign_ready, 1)
                dve.tensor_tensor(dlog[:, :], m12[:, 1, :], m12[:, 0, :], ALU.subtract).then_inc(dlog_ready, 1)

            def take_ranks(L, s):
                dve.wait_ge(rank_done, s + (L * per_group + 1))
                step(dve.tensor_tensor(rk[:, :, :], c1[:, 0, 0:TILES * experts].rearrange("p (t e) -> p t e", t=TILES),
                                       over_t(ecap[:, :]), ALU.add))
                dve.wait_ge(assign_ready, s + (L * per_group + 1))
                step(dve.reduce_sum(arow[:, :], assign[:, :, :].rearrange("p t e -> p e t"), AX.X))
                settle()
                step(dve.tensor_tensor(asum[:, :], asum[:, :], arow[:, :], ALU.add))

            def slots(L, s):
                buffer_free(dve, scattered, 16 * K2, L, s)
                settle()
                step(dve.tensor_tensor(pick[:, :, :, :], oh[:, :, :, :],
                                       rk[:, :, :].unsqueeze(1).to_broadcast([P, 2, TILES, experts]), ALU.mult))
                settle()
                here = pos[:, bass.ds(s, 1), :]
                step(dve.reduce_sum(here.rearrange("p a (k t) -> p (a k) t", k=2), pick[:, :, :, :], AX.X))
                settle()
                dve.tensor_scalar(idx[:, parity(L, s), :], here.rearrange("p a k -> p (a k)"), float(L * NR), None, ALU.add)\
                    .then_inc(idx_ready, 1)

            def weights(L, s):
                c = chunk_of(L, s)
                dve.wait_ge(edl_ready, s + (L * per_group + 1))
                step(dve.tensor_scalar(den[:, :], edl[:, :], 1.0, None, ALU.add))
                settle()
                step(dve.reciprocal(rden[:, :], den[:, :]))
                settle()
                w = [wts[:, k, bass.ds(c * TILES, TILES)] for k in range(2)]
                step(dve.tensor_scalar(w[0], rden[:, :], 0.5, None, ALU.mult))
                step(dve.scalar_tensor_tensor(w[1], edl[:, :], 0.5, rden[:, :], ALU.mult, ALU.mult))

            TAIL_STEPS = 12 + 5 + 4
            ROUTE_STEPS = 2 * TILES + TAIL_STEPS
            COMBINE_STEPS = 2 * TILES
            ATT_STEPS = 2 * TILES + 6 + 2

            def table(L):
                def bc(ap, n):
                    return ap.unsqueeze(1).to_broadcast([ap.shape[0], n, experts])
                routed = slice(L * NB + ROUTED_AT, L * NB + ROUTED_AT + RT)
                dve.wait_ge(count_done, L + 1)
                step(dve.tensor_copy(cnt[:, :], c1[:, 0, 0:experts]))
                step(dve.memset(asum[:, :], 0.0))
                settle()
                step(dve.tensor_scalar(cnt_i[:, :], cnt[:, :], float(BLOCK - 1), None, ALU.add))
                step(dve.tensor_tensor(padf[:, :], cnt[0:1, :], ecap[0:1, :], ALU.add))
                settle()
                step(dve.tensor_scalar(padrow[:, :], padf[:, :], float(L * NR), None, ALU.add))
                step(dve.tensor_scalar(nb_i[:, :], cnt_i[:, :], BLOCK.bit_length() - 1, None, ALU.arith_shift_right))
                settle()
                step(dve.tensor_copy(nb[:, :], nb_i[:, :]))
                settle()
                step(dve.tensor_tensor(cumm[:, :, :], tri[:, :, :], bc(nb[0:1, :], experts), ALU.mult))
                settle()
                step(dve.reduce_sum(cum[:, :], cumm[:, :, :], AX.X))
                settle()
                step(dve.tensor_tensor(le[:, :, :], bc(cum[:, :], RT), nidx[:, :].unsqueeze(2).to_broadcast([1, RT, experts]),
                                       ALU.is_le))
                settle()
                step(dve.reduce_sum(en[:, :], le[:, :, :], AX.X))
                step(dve.tensor_tensor(le2[:, :, :], le[:, :, :], bc(nb[0:1, :], RT), ALU.mult))
                settle()
                step(dve.reduce_sum(cp[:, :], le2[:, :, :], AX.X))
                step(dve.tensor_scalar(ok[:, :], en[:, :], float(experts), float(BLOCK), ALU.is_lt, ALU.mult))
                settle()
                step(dve.tensor_tensor(bi[:, :], nidx[:, :], cp[:, :], ALU.subtract))
                settle()
                step(dve.tensor_tensor(bo[:, :], bi[:, :], ok[:, :], ALU.mult))
                step(dve.tensor_scalar(ro[:, :], en[:, :], float(CAP), float(L * NR), ALU.mult, ALU.add))
                step(dve.tensor_copy(etab[:, routed], en[:, :]))
                settle()
                step(dve.tensor_tensor(rtab[:, routed], ro[:, :], bo[:, :], ALU.add))
                step(dve.memset(hop[:, 0:1], float(ROUTED_AT * BLOCK)))
                step(dve.tensor_scalar(hop[:, 1:experts], nb[:, 0:experts - 1], float(BLOCK), -float(CAP), ALU.mult, ALU.add))
                allpos = pos[:, :, :].rearrange("p c k -> p (c k)")
                n = per_group * K2
                step(dve.tensor_tensor(posge[:, :, :], allpos.unsqueeze(2).to_broadcast([P, n, experts]), bc(ecap[:, :], n), ALU.is_ge))
                settle()
                step(dve.tensor_tensor(posge[:, :, :], posge[:, :, :], bc(hop[:, :], n), ALU.mult))
                settle()
                step(dve.reduce_sum(shift[:, :], posge[:, :, :], AX.X))
                settle()
                g = L % groups
                dve.tensor_tensor(gix[:, g * per_group:(g + 1) * per_group, :].rearrange("p c k -> p (c k)"), allpos, shift[:, :],
                                  ALU.add).then_inc(table_ready, 1)

            TABLE_STEPS = 24

            def note_sums():
                settle()
                dve.tensor_copy(arow[:, 0:1], asum[:, 0:1]).then_inc(sums_ready, 1)

            def combine_choice(L, s, ch, par=0):
                k = s + (L - 2) * per_group
                c = chunk_of(L, s)
                if L < LAST + 2:
                    dve.wait_ge(gathered[par][ch], 16 * TILES if par else (k + 1) * (16 * TILES))
                else:
                    dve.wait_ge(tokens_back[par][ch], 16 * (s // 2 + 1))
                if ch == 1:
                    settle()
                for t in range(TILES):
                    xc = tile_of(c, t)
                    step(dve.scalar_tensor_tensor(xc, yg[:, par, ch * TILES + t, :], wts[:, ch, bass.ds(c * TILES + t, 1)],
                                                  xc, ALU.mult, ALU.add))

            def combine_shared(L, s):
                k = s + (L - 2) * per_group
                par = shared_buffer(L, s)
                if L == 5:
                    dve.wait_ge(shared_back[par], 16 * (s // 2 + 1 + (0 if par else 3 * per_group)))
                else:
                    dve.wait_ge(shared_back[par], k * 16 + 16)
                settle()
                xa = X[:, bass.ds(chunk_of(L, s) * TILES, TILES), :]
                dve.scalar_tensor_tensor(xa, shared_rows(par), 0.5, xa, ALU.mult, ALU.add).then_inc(combined, 1)
                wait_apart(dve, combined, k + (1 + FREE))

            def att_soft1(t):
                dve.wait_ge(scores_done, t + 1)
                step(dve.tensor_tensor(gm[:, :, :], c1[:, :, :], mask[:, :].unsqueeze(1).to_broadcast([P, SEQS, P]), ALU.mult))
                settle()
                step(dve.reduce_sum(hd[:, :, :], gm[:, :, :].rearrange("p b (k i) -> p b i k", i=HEAD), AX.X))
                settle()
                step(dve.reduce_max(hmx[:, :], hd[:, :, :], AX.X))
                settle()
                dve.tensor_tensor(hd2[:, :, :], hd[:, :, :], hmx[:, :].unsqueeze(2).to_broadcast([P, SEQS, HEAD]), ALU.subtract)\
                    .then_inc(hd_ready, 1)

            def att_soft2(t):
                dve.wait_ge(exp_ready, t + 1)
                step(dve.reduce_sum(hsum[:, :], hex_[:, :, :], AX.X))
                settle()
                step(dve.reciprocal(hrec[:, :], hsum[:, :]))
                settle()
                step(dve.tensor_tensor(hp[:, :, :], hex_[:, :, :], hrec[:, :].unsqueeze(2).to_broadcast([P, SEQS, HEAD]), ALU.mult))
                settle()
                for b in range(SEQS):
                    last = dve.tensor_tensor(prob[:, b, :].rearrange("p (k i) -> p k i", i=HEAD),
                                             mask[:, :].rearrange("p (k i) -> p k i", i=HEAD),
                                             hp[:, b, :].unsqueeze(1).to_broadcast([P, P // HEAD, HEAD]), ALU.mult)
                last.then_inc(prob_ready, 1)

            def att_add(L, s, t):
                c = chunk_of(L, s)
                for h, bank in enumerate((c0, c1)):
                    dve.wait_ge(att_done, t * 2 + (h + 1))
                    xa = X[:, bass.ds(c * TILES + h * HALF, HALF), :]
                    dve.tensor_tensor(xa, bank[:, :, :], xa, ALU.add).then_inc(att_added, 1)
                wait_apart(dve, att_added, t * 2 + 2)

            ATT_STEPS -= 2

            def take_xT(n, u):
                dve.wait_ge(turned, n + (1 + FREE))
                dve.tensor_copy(xT[:, u % RING, :, :].rearrange("p h s -> p (h s)"),
                                tps[:, :, :, :].rearrange("p h a b -> p (h a b)")).then_inc(xT_ready, 1)

            def keep_ids(n, u):
                wait_apart(dve, y_ready, n + (FREE - 3))
                step(dve.tensor_copy(idf32[:, u % 2, :], row_ids(xin[:, u % RING, :, :])))
                settle()
                step(dve.tensor_scalar(idhop[:, u % 2, :], idf32[:, u % 2, :], float(UNUSED), float(u % RING * BLOCK), ALU.is_ge, ALU.mult))
                settle()
                dve.tensor_tensor(oid[:, u % (2 * RING), :], idhop[:, u % 2, :], idf32[:, u % 2, :], ALU.add).then_inc(ids_kept, 1)

            def split_block(n, u):
                g = u % 2
                dve.wait_ge(hi0_done, n + 1)
                dve.tensor_tensor(gl[:, g, 0:2, :], g32[:, g, 0:2, :], gh[:, g, 0:2, :], ALU.subtract).then_inc(lo_done, 1)
                dve.wait_ge(hi1_done, n + 1)
                dve.tensor_tensor(gl[:, g, 2:4, :], g32[:, g, 2:4, :], gh[:, g, 2:4, :], ALU.subtract).then_inc(lo_done, 1)

            dve.sem_inc(xT_ready, FREE)
            dve.wait_ge(const_ready, 2)
            dve.wait_ge(xload[0], 16)
            for k in range(2):
                dve.tensor_scalar(row_ids(xhl[:, k, :, :]), tokid[:, k, :], 0.0, None, ALU.add)
            stats(0, norm_count(0, 0, 1))
            for s in range(per_group - 1):
                n1 = norm_count(0, s, 1)
                normalise(s, n1)
                split_low(0, s)
                if s == 2:
                    split_block(0, 0)
                    take_xT(2, 2)
                if s > 0:
                    for n in batch(s):
                        weights_low(n)
                if s == 0:
                    dve.wait_ge(aload, 160)
                route(0, s)
                take_ranks(0, s)
                slots(0, s)
                dve.wait_ge(xload[s + 1], 16)
                stats(s + 1, n1 + 1)
                weights(0, s)
                if s == 0:
                    for n in batch(s):
                        weights_low(n)
                if s == 1:
                    take_xT(0, 0)
                    take_xT(1, 1)
            split_block(1, 1)
            total = (per_group - 1) * ROUTE_STEPS + 2 * TILES
            assert Order.n == total, (Order.n, total)
            dve.wait_ge(xload[per_group], 16 * per_group)

            def blocks_and_chunks(L, s):
                n0 = norm_count(L, s, 0)
                n1 = norm_count(L, s, 1)
                t_ = s + (L - 2) * per_group
                c = chunk_of(L, s)
                tail = tail_of(L, s)
                at = plan(L, s)

                def chunk_part(h):
                    if at.get("last_norm") == h:
                        normalise(per_group - 1, norm_count(0, per_group - 1, 1))
                    if at.get("last_split") == h:
                        split_low(0, per_group - 1)
                        for n in batch(per_group - 1):
                            weights_low(n)
                    if at.get("last_expert") == h:
                        weights_low(NX - 1)
                    if at.get("route") == h:
                        route(*tail)
                    if at.get("take_ranks") == h:
                        take_ranks(*tail)
                    if at.get("slots") == h:
                        slots(*tail)
                    if at.get("weights") == h:
                        weights(*tail)
                    if at.get("combine0") == h:
                        combine_choice(L, combined_in(L, s), 0)
                    if at.get("combine1") == h:
                        combine_choice(L, combined_in(L, s), 1)
                    if at.get("combine2") == h:
                        combine_shared(L, combined_in(L, s))
                    if at.get("stats0") == h:
                        stats(c, n0)
                    if at.get("count") == h:
                        note_sums()
                    if at.get("table") == h:
                        table(L - 1)
                    if at.get("norm0") == h:
                        normalise(c, n0)
                    if at.get("soft1") == h:
                        att_soft1(t_)
                    if at.get("soft2") == h:
                        att_soft2(t_)
                    if at.get("out") == h:
                        att_add(L, s, t_)
                    if at.get("stats1") == h:
                        stats(c, n1)
                    if at.get("norm1") == h:
                        normalise(c, n1)
                    if at.get("split") == h:
                        split_low(L, s)

                for u in range(STEPS):
                    n = s * STEPS + ((L - 1) * NB + u)
                    take_xT(n + 3, u + 3)
                    if L == LAST + 1 and (not isinstance(s, int) or u + 3 >= STEPS):
                        keep_ids(n + 3, u + 3)
                    chunk_part(2 * u)
                    split_block(n + 2, u + 2)
                    chunk_part(2 * u + 1)

            CHUNK_STEPS = {1: ROUTE_STEPS, 2: ROUTE_STEPS + COMBINE_STEPS + ATT_STEPS,
                           3: ROUTE_STEPS + COMBINE_STEPS + ATT_STEPS + 3, 4: COMBINE_STEPS + 2 * STEPS}
            FIRST_STEPS = {1: ROUTE_STEPS + TABLE_STEPS,
                           2: ROUTE_STEPS + COMBINE_STEPS + ATT_STEPS + TABLE_STEPS,
                           3: ROUTE_STEPS + COMBINE_STEPS + ATT_STEPS + TABLE_STEPS + 3,
                           4: TAIL_STEPS + TABLE_STEPS + 2 * 3}
            for L in range(1, 5):
                per = CHUNK_STEPS[L]
                Order.base, Order.n = total, 0
                blocks_and_chunks(L, 0)
                assert Order.n == FIRST_STEPS[L], (L, Order.n, FIRST_STEPS[L])
                total += FIRST_STEPS[L]
                with dve.Fori(1, per_group) as s:
                    Order.base, Order.n = s * per + (total - per), 0
                    blocks_and_chunks(L, s)
                    assert Order.n == per, (L, Order.n, per)
                total += (per_group - 1) * per
            for L, s in [(4, per_group - 1)] + [(5, s) for s in range(per_group)]:
                Order.base, Order.n = total, 0
                for choice in range(2):
                    combine_choice(L, s, choice, s % 2 if L == 5 else 1)
                combine_shared(L, s)
                total += COMBINE_STEPS


_INS = ['L0_attn_x', 'L0_attn_Wq', 'L0_attn_Wk', 'L0_attn_Wv', 'L0_attn_Wo', 'L0_ffn_gate_w', 'L0_ffn_gate_b',
        'L0_ffn_w1', 'L0_ffn_b1', 'L0_ffn_w2', 'L0_ffn_b2', 'L0_ffn_ws1', 'L0_ffn_bs1', 'L0_ffn_ws2', 'L0_ffn_bs2']


def kernel(**inputs):
    import numpy as _np
    import concourse.bacc as _bacc
    from concourse import mybir as _mybir
    from concourse.bass_utils import run_bass_kernel_spmd as _run

    nc = _bacc.Bacc("TRN2", target_bir_lowering=False, num_devices=1)
    arrays, args = {}, []
    for name in _INS:
        a = _np.ascontiguousarray(inputs[name])
        arrays[f"in_{name}_dram"] = a
        args.append(nc.dram_tensor(f"in_{name}_dram", a.shape, _mybir.dt.from_np(a.dtype), kind="ExternalInput").ap())
    shape = arrays["in_L0_attn_x_dram"].shape
    args.append(nc.dram_tensor("out_0_dram", shape, _mybir.dt.float32, kind="ExternalOutput").ap())
    macaron_block(nc, *args)
    r = _run(nc, [arrays], core_ids=[0])
    return r.results[0]["out_0_dram"]
```
